# Optimizing a Trainium2 kernel written in Bass

```python
import numpy as np
import jax
import jax.numpy as jnp

def _softmax(x, axis=-1):
    return jax.nn.softmax(x, axis=axis)

def _gelu(x):
    return jax.nn.gelu(x, approximate=True)

def _silu(x):
    return jax.nn.silu(x)

def _sigmoid(x):
    return jax.nn.sigmoid(x)

def _layernorm(x, axis=-1, eps=1e-05):
    m = jnp.mean(x, axis=axis, keepdims=True)
    v = jnp.var(x, axis=axis, keepdims=True)
    return (x - m) / jnp.sqrt(v + eps)

def _scatter_add(tgt, idx, src, axis=0):
    return tgt.at[idx].add(src)

def _segment_sum(src, seg, n):
    return jax.ops.segment_sum(src, seg, n)
kernel_name = 'mk_decoder_preln_d1_seqx_r8_83e1f4'

def setup_inputs(seed: int=0):
    np.random.seed(seed)
    _w = jnp.asarray

    def _rec_inputs():
        import jax
        import jax.numpy as jnp
        _rk = jax.random.key(seed)
        x = 7.22e-05 + 1 * jax.random.normal(jax.random.fold_in(_rk, 1), (64, 64, 256), jnp.float32)
        _lenS = 64 - jax.random.randint(jax.random.fold_in(_rk, 7), (64,), 0, max(1, 64 // 4) + 1, jnp.int32)
        _lenS2 = 64 - jax.random.randint(jax.random.fold_in(_rk, 8), (64,), 0, max(1, 64 // 4) + 1, jnp.int32)
        _ctx_2048P = jax.random.normal(jax.random.fold_in(_rk, 11), (64, 16, 256), jnp.float32)
        _ctx_2048c = jax.random.dirichlet(jax.random.fold_in(_rk, 511), 0.3 * jnp.ones((16,), jnp.float32), (64, 64))
        _ctx_2048t = jnp.einsum('bsk,bkd->bsd', _ctx_2048c, _ctx_2048P)
        _ctx_2048t = _ctx_2048t * jax.lax.rsqrt(jnp.mean(jnp.square(_ctx_2048t)) + 1e-12) * 0.953939
        ctx_2048 = 4.13588e-05 + 0.999923 * (_ctx_2048t + 0.3 * jax.random.normal(jax.random.fold_in(_rk, 611), (64, 64, 256), jnp.float32))
        return (x, ctx_2048)
    x, ctx_2048 = _rec_inputs()

    def _L0_attn_setup():
        import math
        import jax, jax.numpy as jnp
        import numpy as np
        H = 16
        HKV = 4
        HD = 128
        BASE = 10000.0

        def _rope_tables(L):
            inv_freq = 1.0 / BASE ** (jnp.arange(0, HD, 2, dtype=jnp.float32) / HD)
            pos = jnp.arange(L, dtype=jnp.float32)
            freqs = pos[:, None] * inv_freq[None, :]
            emb = jnp.concatenate([freqs, freqs], axis=-1)
            return (jnp.cos(emb)[None, :, None, :], jnp.sin(emb)[None, :, None, :])
        key = jax.random.key(seed)
        ks = jax.random.split(key, 5)
        B, L, D = (2, 256, 256)
        s = 0.02
        return {'x': jax.random.normal(ks[0], (B, L, D), jnp.float32), 'Wq': jax.random.normal(ks[1], (D, H * HD), jnp.float32) * s, 'Wk': jax.random.normal(ks[2], (D, HKV * HD), jnp.float32) * s, 'Wv': jax.random.normal(ks[3], (D, HKV * HD), jnp.float32) * s, 'Wo': jax.random.normal(ks[4], (H * HD, D), jnp.float32) * s}
    _L0_attn_all = _L0_attn_setup()
    _L0_attn_in = {k: v for k, v in _L0_attn_all.items() if k in ('Wq', 'Wk', 'Wv', 'Wo')}
    del _L0_attn_all

    def _L0_xattn_setup():
        import jax, jax.numpy as jnp
        import numpy as np
        N_HEAD = 8
        key = jax.random.key(seed)
        k1, k2, k3 = jax.random.split(key, 3)
        B, D, L = (4, 128, 256)
        q = jax.random.normal(k1, (B, D, L), dtype=jnp.float32)
        k = jax.random.normal(k2, (B, D, L), dtype=jnp.float32)
        v = jax.random.normal(k3, (B, D, L), dtype=jnp.float32)
        gamma = jnp.ones((), dtype=jnp.float32)
        return {'q': q, 'k': k, 'v': v, 'gamma': gamma}
    _L0_xattn_all = _L0_xattn_setup()
    _L0_xattn_in = {k: v for k, v in _L0_xattn_all.items() if k in ('gamma',)}
    del _L0_xattn_all

    def _L0_ffn_setup():
        import jax, jax.numpy as jnp
        import numpy as np
        E = 8
        TOP_K = 2
        H = 256
        I_MOE = 176
        I_SH = 704
        B, S = (2, 256)

        def _moe_forward(hidden_states, router_weight, gate_up_proj, down_proj, sh_gate_w, sh_up_w, sh_down_w, shared_gate_w):
            b, s, h = hidden_states.shape
            x = hidden_states.reshape(-1, h)
            shared = jnp.einsum('ti,hi->th', jax.nn.silu(x @ sh_gate_w.T) * (x @ sh_up_w.T), sh_down_w)
            logits = x @ router_weight.T
            probs = jax.nn.softmax(logits.astype(jnp.float32), axis=-1)
            top_v, top_i = jax.lax.top_k(probs, TOP_K)
            top_v = top_v / top_v.sum(axis=-1, keepdims=True)
            combine = (jax.nn.one_hot(top_i, E, dtype=top_v.dtype) * top_v[..., None]).sum(axis=1)
            out = jnp.zeros_like(x)
            for e in range(E):
                gu = x @ gate_up_proj[e].T
                gate, up = (gu[:, :I_MOE], gu[:, I_MOE:])
                cur = jax.nn.silu(gate) * up @ down_proj[e].T
                out = out + cur * combine[:, e:e + 1]
            out = out + jax.nn.sigmoid(x @ shared_gate_w.T) * shared
            return out.reshape(b, s, h)
        key = jax.random.key(seed)
        ks = jax.random.split(key, 8)
        scale = 0.02
        return {'hidden_states': jax.random.normal(ks[0], (B, S, H), dtype=jnp.float32), 'router_weight': jax.random.normal(ks[1], (E, H), dtype=jnp.float32) * scale, 'gate_up_proj': jax.random.normal(ks[2], (E, 2 * I_MOE, H), dtype=jnp.float32) * scale, 'down_proj': jax.random.normal(ks[3], (E, H, I_MOE), dtype=jnp.float32) * scale, 'sh_gate_w': jax.random.normal(ks[4], (I_SH, H), dtype=jnp.float32) * scale, 'sh_up_w': jax.random.normal(ks[5], (I_SH, H), dtype=jnp.float32) * scale, 'sh_down_w': jax.random.normal(ks[6], (H, I_SH), dtype=jnp.float32) * scale, 'shared_gate_w': jax.random.normal(ks[7], (1, H), dtype=jnp.float32) * scale}
    _L0_ffn_all = _L0_ffn_setup()
    _L0_ffn_in = {k: v for k, v in _L0_ffn_all.items() if k in ('router_weight', 'gate_up_proj', 'down_proj', 'sh_gate_w', 'sh_up_w', 'sh_down_w', 'shared_gate_w')}
    del _L0_ffn_all
    return {'x': x, 'ctx_2048': ctx_2048, 'L0_attn_Wq': _L0_attn_in['Wq'], 'L0_attn_Wk': _L0_attn_in['Wk'], 'L0_attn_Wv': _L0_attn_in['Wv'], 'L0_attn_Wo': _L0_attn_in['Wo'], 'L0_xattn_gamma': _L0_xattn_in['gamma'], 'L0_ffn_router_weight': _L0_ffn_in['router_weight'], 'L0_ffn_gate_up_proj': _L0_ffn_in['gate_up_proj'], 'L0_ffn_down_proj': _L0_ffn_in['down_proj'], 'L0_ffn_sh_gate_w': _L0_ffn_in['sh_gate_w'], 'L0_ffn_sh_up_w': _L0_ffn_in['sh_up_w'], 'L0_ffn_sh_down_w': _L0_ffn_in['sh_down_w'], 'L0_ffn_shared_gate_w': _L0_ffn_in['shared_gate_w']}

def reference(x, ctx_2048, L0_attn_Wq, L0_attn_Wk, L0_attn_Wv, L0_attn_Wo, L0_xattn_gamma, L0_ffn_router_weight, L0_ffn_gate_up_proj, L0_ffn_down_proj, L0_ffn_sh_gate_w, L0_ffn_sh_up_w, L0_ffn_sh_down_w, L0_ffn_shared_gate_w):
    import jax
    import jax.numpy as jnp

    def _L0_attn_ref(x, Wq, Wk, Wv, Wo):
        import math
        import jax, jax.numpy as jnp
        import numpy as np
        H = 16
        HKV = 4
        HD = 128
        BASE = 10000.0

        def _rope_tables(L):
            inv_freq = 1.0 / BASE ** (jnp.arange(0, HD, 2, dtype=jnp.float32) / HD)
            pos = jnp.arange(L, dtype=jnp.float32)
            freqs = pos[:, None] * inv_freq[None, :]
            emb = jnp.concatenate([freqs, freqs], axis=-1)
            return (jnp.cos(emb)[None, :, None, :], jnp.sin(emb)[None, :, None, :])
        B, L, D = x.shape
        q = (x @ Wq).reshape(B, L, H, HD)
        k = (x @ Wk).reshape(B, L, HKV, HD)
        v = (x @ Wv).reshape(B, L, HKV, HD)
        rep = H // HKV
        k = jnp.repeat(k, rep, axis=2)
        v = jnp.repeat(v, rep, axis=2)
        cos, sin = _rope_tables(L)
        q = q * cos + jnp.roll(q, shift=1, axis=-1) * sin
        k = k * cos + jnp.roll(k, shift=1, axis=-1) * sin
        q = q.transpose(0, 2, 1, 3)
        k = k.transpose(0, 2, 1, 3)
        v = v.transpose(0, 2, 1, 3)
        attn = jnp.einsum('bhqd,bhkd->bhqk', q, k) / math.sqrt(HD)
        attn = jax.nn.softmax(attn, axis=-1)
        out = jnp.einsum('bhqk,bhkd->bhqd', attn, v)
        out = out.transpose(0, 2, 1, 3).reshape(B, L, H * HD)
        return out @ Wo

    def _L0_xattn_ref(q, k, v, gamma):
        import jax, jax.numpy as jnp
        import numpy as np
        N_HEAD = 8
        B, Dq, Lq = q.shape
        Dv, Lk = (v.shape[-2], v.shape[-1])
        h = N_HEAD
        dq = Dq // h
        dv = Dv // h
        qh = q.reshape(B, h, dq, Lq)
        kh = k.reshape(B, h, dq, Lk)
        vh = v.reshape(B, h, dv, Lk)
        scale = 1.0 / jnp.sqrt(jnp.asarray(dq, dtype=q.dtype))
        qk = jnp.einsum('bhdq,bhdl->bhql', qh, kh) * scale
        sm = jax.nn.softmax(qk, axis=-1)
        ret = jnp.einsum('bhql,bhdl->bhdq', sm, vh)
        ret = ret.reshape(B, Dv, Lq)
        return gamma * ret

    def _L0_ffn_ref(hidden_states, router_weight, gate_up_proj, down_proj, sh_gate_w, sh_up_w, sh_down_w, shared_gate_w):
        import jax, jax.numpy as jnp
        import numpy as np
        E = 8
        TOP_K = 2
        H = 256
        I_MOE = 176
        I_SH = 704
        B, S = (2, 256)

        def _moe_forward(hidden_states, router_weight, gate_up_proj, down_proj, sh_gate_w, sh_up_w, sh_down_w, shared_gate_w):
            b, s, h = hidden_states.shape
            x = hidden_states.reshape(-1, h)
            shared = jnp.einsum('ti,hi->th', jax.nn.silu(x @ sh_gate_w.T) * (x @ sh_up_w.T), sh_down_w)
            logits = x @ router_weight.T
            probs = jax.nn.softmax(logits.astype(jnp.float32), axis=-1)
            top_v, top_i = jax.lax.top_k(probs, TOP_K)
            top_v = top_v / top_v.sum(axis=-1, keepdims=True)
            combine = (jax.nn.one_hot(top_i, E, dtype=top_v.dtype) * top_v[..., None]).sum(axis=1)
            out = jnp.zeros_like(x)
            for e in range(E):
                gu = x @ gate_up_proj[e].T
                gate, up = (gu[:, :I_MOE], gu[:, I_MOE:])
                cur = jax.nn.silu(gate) * up @ down_proj[e].T
                out = out + cur * combine[:, e:e + 1]
            out = out + jax.nn.sigmoid(x @ shared_gate_w.T) * shared
            return out.reshape(b, s, h)
        return _moe_forward(hidden_states, router_weight, gate_up_proj, down_proj, sh_gate_w, sh_up_w, sh_down_w, shared_gate_w)
    x = x + _L0_attn_ref(_layernorm(x, axis=-1), L0_attn_Wq, L0_attn_Wk, L0_attn_Wv, L0_attn_Wo)
    x = x + _L0_xattn_ref(_layernorm(x, axis=-1), ctx_2048, ctx_2048, L0_xattn_gamma)
    x = x + _L0_ffn_ref(_layernorm(x, axis=-1), L0_ffn_router_weight, L0_ffn_gate_up_proj, L0_ffn_down_proj, L0_ffn_sh_gate_w, L0_ffn_sh_up_w, L0_ffn_sh_down_w, L0_ffn_shared_gate_w)
    return x

_drawn_inputs = setup_inputs


def setup_inputs(seed=0):
    import zlib

    import numpy as np

    out = dict(_drawn_inputs(seed))
    spreads = {}
    factors = {'L0_attn_Wq': 8.0,
     'L0_attn_Wk': 8.0,
     'L0_ffn_router_weight': 8.0,
     'L0_ffn_gate_up_proj': 7.826,
     'L0_ffn_down_proj': 7.833,
     'L0_ffn_sh_gate_w': 5.606,
     'L0_ffn_sh_up_w': 5.529,
     'L0_ffn_sh_down_w': 5.554,
     'L0_ffn_shared_gate_w': 8.0}
    for name, (base, spread) in spreads.items():
        noise = np.random.default_rng([zlib.crc32(name.encode()), seed]).standard_normal(out[name].shape)
        drawn = base * np.exp(spread * noise) if base else spread * noise
        out[name] = jnp.asarray(drawn.astype(out[name].dtype))
    for name, factor in factors.items():
        out[name] = (out[name] * factor).astype(out[name].dtype)
    return out
```

```python
from contextlib import ExitStack

import numpy as np

import concourse.bass as bass
from concourse import mybir

F32 = mybir.dt.float32
F16 = mybir.dt.float16
ALU = mybir.AluOpType
ACT = mybir.ActivationFunctionType
AX = mybir.AxisListType

P = 128
SEQS, L, D = 64, 64, 256
T = SEQS * L
TILES = T // P
KT = D // P
H, HKV, HD = 16, 4, 128
REP = H // HKV
GT = 4
GN = GT * P
GROUPS = TILES // GT
EPS = 1e-5

S_X, S_W, S_VO = 64.0, 256.0, 2048.0
S_V = 64.0
S_Y, S_C = 16.0, 16.0
S_H, S_CMB = 8.0, 256.0

XH, XD, XJ = 8, 8, 4
XS = XH // XJ
MAXROW = 3 * XD

E, I_MOE, I_SH = 8, 176, 704
MT = -(-(E * I_MOE + I_SH) // P)
HID = MT * P
WC_CHUNKS = 14
CH = 1024
GU_OFF, DN_OFF, RT_OFF = 0, KT * 2 * HID, KT * 2 * HID + MT * D


def wait_apart(eng, setup, *waits):
    for _, count in waits:
        if not isinstance(count, int):
            eng.compute_val(count)
    eng.wait_ge(*setup)
    for sem, count in waits:
        eng.wait_ge(sem, count)


def ln_statistics(nc, dve, tiles, mv, stats, step, done, group, setup):
    n = len(tiles)
    for j, src in enumerate(tiles):
        nc.vector.bn_stats(stats[:, j, :], src).then_inc(step, 1)
    for j in range(n):
        wait_apart(dve, setup, (step, n * group + j + 1))
        nc.vector.bn_aggr(mv[:, j, :], stats[:, j, :]).then_inc(done, 1)


def ln_rstd(nc, pool, mv, rstd, half, have, count, added, nth, done, setup, scale=1.0, waits=()):
    wait_apart(pool, setup, (have, count), *waits)
    nc.gpsimd.tensor_scalar(rstd[:, :], mv[:, :, 1], EPS, scale ** -2, ALU.add, ALU.mult).then_inc(added, 1)
    pool.wait_ge(added, nth)
    nc.gpsimd.tensor_tensor(rstd[:, :], rstd[:, :], half, ALU.pow).then_inc(done, 1)


def ln_normalise(nc, dve, src, dst, mv, rstd, j, done):
    nc.vector.tensor_scalar(dst, src, mv[:, j, 0:1], rstd[:, j:j + 1], ALU.subtract, ALU.mult).then_inc(done, 1)


def matmul3(nc, out, stat, mov, start, stop):
    nc.tensor.matmul(out, stat[0], mov[0], start=start, stop=False)
    nc.tensor.matmul(out, stat[0], mov[1], start=False, stop=False)
    return nc.tensor.matmul(out, stat[1], mov[0], start=False, stop=stop)


def block_a(nc, X, ident, a):
    with ExitStack() as ctx:
        def sb(name, shape, dt=F32):
            return ctx.enter_context(nc.sbuf_tensor(name, shape, dt))

        def sem(name):
            return ctx.enter_context(nc.semaphore(name))

        NCH = 10
        WH = sb("a_wh", [P, NCH, CH], F16)
        WL = sb("a_wl", [P, NCH, CH], F16)
        aTh = sb("a_ath", [P, H, GN], F16)
        aTl = sb("a_atl", [P, H, GN], F16)
        stage = aTh[:, :, :].rearrange("p h n -> p (h n)").bitcast(F32).rearrange("p (s c) -> p s c", c=CH)
        NST = 4
        xhat = sb("a_xhat", [P, GT, D])
        stats = sb("a_stats", [P, GT, 6])
        mv = sb("a_mv", [P, GT, 2])
        rstd = sb("a_rstd", [P, GT])
        half = sb("a_half", [P, GT])
        xTh = sb("a_xth", [P, KT, GN], F16)
        xTl = sb("a_xtl", [P, KT, GN], F16)
        tabq = sb("a_tabq", [P, 2, L])
        tabk = sb("a_tabk", [P, 2, HD])
        kmul = sb("a_kmul", [P, 2, 2, HKV, HD])
        kext = sb("a_kext", [P, 2, HKV, HD + 1])
        kT = sb("a_kt", [P, GT, HKV, 2, P])
        V = sb("a_v", [P, 2, GT, HKV * HD])
        qCS = sb("a_qcs", [P, 2, 2, REP, GN])
        st = sb("a_st", [P, 2, 512])
        pr = sb("a_pr", [P, 2, 512])
        pn = sb("a_pn", [P, 2, 512])
        pT = sb("a_pt", [P, 2, 512])
        sm = sb("a_sm", [P, 2, 3, 8])
        B = [ctx.enter_context(nc.psum_tensor(f"a_bank{n}", [P, 512], F32)) for n in range(8)]

        wa_in = [sem(f"a_wa_in{n}") for n in range(NST)]
        tab_in, w_hi, w_lo, v_zero = sem("a_tab_in"), sem("a_w_hi"), sem("a_w_lo"), sem("a_v_zero")
        x_in = [sem(f"a_x_in{n}") for n in range(GROUPS)]
        ln_add = sem("a_ln_add")
        ln_st, ln_mv, ln_rs, xhat_ok = sem("a_ln_st"), sem("a_ln_mv"), sem("a_ln_rs"), sem("a_xhat_ok")
        xtr, xT_hi, xT_lo = sem("a_xtr"), sem("a_xt_hi"), sem("a_xt_lo")
        k_proj, v_proj, q_proj = sem("a_k_proj"), sem("a_v_proj"), sem("a_q_proj")
        k_mul, k_ext, k_tr, k_T, v_ok = sem("a_k_mul"), sem("a_k_ext"), sem("a_k_tr"), sem("a_k_t"), sem("a_v_ok")
        k_wrap = sem("a_k_wrap")
        q_rope = sem("a_q_rope")
        s_mm, s_copy, s_tr, s_max, s_sub, s_exp = (sem("a_" + n) for n in ("s_mm", "s_copy", "s_tr", "s_max", "s_sub", "s_exp"))
        s_sum, s_rec, p_ok, p_tr, p_T = (sem("a_" + n) for n in ("s_sum", "s_rec", "p_ok", "p_tr", "p_t"))
        pv, a_hi, a_lo, wo, x_new = (sem("a_" + n) for n in ("pv", "a_hi", "a_lo", "wo", "x_new"))

        block = ctx.enter_context(nc.Block())
        LAST = GROUPS - 1
        SETUP = (v_zero, 3)

        def in_loop(eng, body):
            body(0, False)
            with eng.Fori(1, LAST) as i:
                body(i, False)
            body(LAST, True)

        def next_xT_hi(act, base):
            for kt in range(KT):
                act.wait_ge(xtr, base + kt + 1)
                nc.scalar.activation(xTh[:, kt], B[6 + kt][:, :], ACT.Copy, scale=S_X).then_inc(xT_hi, 1)

        def head_cols(t, kv, p):
            return t[:, REP * kv:REP * kv + REP, p * P:(p + 1) * P].rearrange("p h (b q) -> p b h q", b=2)

        def pv_cols(bank):
            return bank[:, :].rearrange("p (b h q) -> p b h q", b=2, h=REP)

        @block.sync
        def _(sp):
            xg = a["x"].rearrange("(g t p) d -> g p t d", p=P, t=GT)
            sp.dma_start(X[:, 0:GT, :], xg[0]).then_inc(x_in[0], 16)
            sp.dma_start(tabq[:, :, :], a["tabq"].rearrange("p (a l) -> p a l", a=2)).then_inc(tab_in, 16)
            sp.dma_start(tabk[:, :, :], a["tabk"].rearrange("p (a l) -> p a l", a=2)).then_inc(tab_in, 16)
            sp.dma_start(ident[:, :], a["ident"]).then_inc(tab_in, 16)
            for c in range(NCH):
                if c >= NST:
                    sp.wait_ge(w_lo, c - NST + 1)
                sp.dma_start(stage[:, c % NST, :], a["wA"][c]).then_inc(wa_in[c % NST], 16)
                if c < GROUPS - 1:
                    sp.dma_start(X[:, (c + 1) * GT:(c + 2) * GT, :], xg[c + 1]).then_inc(x_in[c + 1], 16)

        @block.gpsimd
        def _(pool):
            nc.gpsimd.memset(half[:, :], -0.5).then_inc(v_zero, 1)
            for s in range(2):
                pool.wait_ge(v_zero, s + 1)
                nc.gpsimd.memset(V[64 * (1 - s):64 * (1 - s) + 64, s, :, :], 0.0).then_inc(v_zero, 1)

            pool.wait_ge(v_zero, 3)
            ln_rstd(nc, pool, mv, rstd, half[:, :], ln_mv, GT, ln_add, 1, ln_rs, SETUP)

            def body(i, last):
                def rotate_k(j):
                    pool.wait_ge(k_mul, 4 * i + j + 1)
                    if j >= 2:
                        pool.wait_ge(k_tr, 8 * i + 2 * (j - 1))
                    else:
                        pool.wait_ge(k_tr, 8 * i)
                    b = j % 2
                    nc.gpsimd.tensor_tensor(kext[:, b, :, 0:HD], kmul[:, b, 0], kmul[:, b, 1], ALU.add).then_inc(k_wrap, 1)
                    wait_apart(pool, SETUP, (k_wrap, 4 * i + j + 1))
                    nc.gpsimd.tensor_copy(kext[:, b, :, HD:HD + 1], kext[:, b, :, 0:1]).then_inc(k_ext, 1)

                def normalise(kv):
                    for u in range(2):
                        n = 8 * i + 2 * kv + u
                        pool.wait_ge(s_rec, n + 1)
                        if kv >= 1:
                            pool.wait_ge(p_tr, n - 1)
                        else:
                            pool.wait_ge(p_tr, 8 * i)
                        nc.gpsimd.tensor_tensor(pn[:, u].rearrange("p (g k) -> p g k", k=L), pr[:, u].rearrange("p (g k) -> p g k", k=L),
                                                sm[:, u, 2, :].unsqueeze(2).to_broadcast([P, 8, L]), ALU.mult).then_inc(p_ok, 1)

                for j in range(GT):
                    rotate_k(j)
                for kv in range(HKV - 1):
                    normalise(kv)
                if not last:
                    used = (xhat_ok, GT * i + GT)
                    ln_rstd(nc, pool, mv, rstd, half[:, :], ln_mv, GT * i + 2 * GT, ln_add, i + 2, ln_rs, SETUP, waits=[used])
                normalise(HKV - 1)

            in_loop(pool, body)

        @block.scalar
        def _(act):
            for c in range(NCH):
                act.wait_ge(wa_in[c % NST], 16 * (c // NST + 1))
                scale = S_VO if c == 1 or c >= 6 else S_W
                nc.scalar.activation(WH[:, c], stage[:, c % NST], ACT.Copy, scale=scale).then_inc(w_hi, 1)
                if c == 1:
                    next_xT_hi(act, 0)
            act.wait_ge(w_lo, NCH)
            act.wait_ge(v_zero, 3)

            def body(i, last):
                def copy_v(j):
                    act.wait_ge(v_proj, 4 * i + j + 1)
                    act.wait_ge(pv, 16 * i)
                    for s in range(2):
                        rows = slice(64 * s, 64 * s + 64)
                        ins = nc.scalar.activation(V[rows, s, j, :], B[1][rows, :], ACT.Copy, scale=S_V / (S_X * S_VO))
                    ins.then_inc(v_ok, 1)

                def copy_kT(j):
                    act.wait_ge(s_mm, 8 * i)
                    for b in range(2):
                        act.wait_ge(k_tr, 8 * i + 2 * j + b + 1)
                        nc.scalar.activation(kT[:, j, 2 * b:2 * b + 2].rearrange("p a c n -> p (a c n)"), B[4 + b][:, :], ACT.Copy).then_inc(k_T, 1)

                def copy_scores(kv):
                    for u in range(2):
                        n = 8 * i + 2 * kv + u
                        act.wait_ge(s_mm, n + 1)
                        if kv >= 1:
                            act.wait_ge(s_tr, n - 1)
                        else:
                            act.wait_ge(s_tr, 8 * i)
                        nc.scalar.activation(st[:, u], B[2 + u][:, :], ACT.Copy).then_inc(s_copy, 1)

                def exps(kv):
                    for u in range(2):
                        act.wait_ge(s_sub, 8 * i + 2 * kv + u + 1)
                        nc.scalar.activation(pr[:, u], pr[:, u], ACT.Exp).then_inc(s_exp, 1)

                def copy_pT(kv):
                    for u in range(2):
                        n = 8 * i + 2 * kv + u
                        act.wait_ge(p_tr, n + 1)
                        if kv >= 1:
                            act.wait_ge(pv, 2 * (n - 1))
                        else:
                            act.wait_ge(pv, 16 * i)
                        nc.scalar.activation(pT[:, u], B[4 + u][:, :], ACT.Copy).then_inc(p_T, 1)

                def out_hi(kv):
                    if kv == 0:
                        act.wait_ge(wo, 4 * i)
                    for p in range(GT):
                        act.wait_ge(pv, 16 * i + 4 * kv + p + 1)
                        nc.scalar.activation(head_cols(aTh, kv, p), pv_cols(B[6 + p % 2]), ACT.Copy).then_inc(a_hi, 1)

                copy_v(0)
                copy_v(1)
                copy_v(2)
                copy_kT(0)
                copy_v(3)
                for j in range(1, GT):
                    copy_kT(j)
                copy_scores(0)
                for kv in range(1, HKV):
                    exps(kv - 1)
                    copy_pT(kv - 1)
                    copy_scores(kv)
                    out_hi(kv - 1)
                exps(HKV - 1)
                copy_pT(HKV - 1)
                out_hi(HKV - 1)
                if not last:
                    next_xT_hi(act, 2 * i + 2)

            in_loop(act, body)

        @block.vector
        def _(dve):
            def tiles(group):
                return [X[:, bass.ds(GT * group + j, 1), :].rearrange("p o d -> p (o d)") for j in range(GT)]

            def normalise(group):
                dve.wait_ge(ln_rs, group + 1)
                for j, src in enumerate(tiles(group)):
                    ln_normalise(nc, dve, src, xhat[:, j, :], mv, rstd, j, xhat_ok)

            def xT_lo_parts(base):
                for kt in range(KT):
                    dve.wait_ge(xT_hi, base + kt + 1)
                    nc.vector.scalar_tensor_tensor(xTl[:, kt], B[6 + kt][:, :], S_X, xTh[:, kt], ALU.mult, ALU.subtract).then_inc(xT_lo, 1)

            dve.wait_ge(x_in[0], 16)
            ln_statistics(nc, dve, tiles(0), mv, stats, ln_st, ln_mv, 0, SETUP)
            normalise(0)
            for c in range(NCH):
                dve.wait_ge(w_hi, c + 1)
                scale = S_VO if c == 1 or c >= 6 else S_W
                nc.vector.scalar_tensor_tensor(WL[:, c], stage[:, c % NST], scale, WH[:, c], ALU.mult, ALU.subtract).then_inc(w_lo, 1)
                if c == 1:
                    xT_lo_parts(0)
            dve.wait_ge(tab_in, 48)
            for g in range(1, GROUPS):
                dve.wait_ge(x_in[g], 16)

            def body(i, last):
                def multiply_k(j):
                    b = j % 2
                    dve.wait_ge(k_proj, 4 * i + j + 1)
                    if j >= 2:
                        dve.wait_ge(k_wrap, 4 * i + j - 1)
                    else:
                        dve.wait_ge(k_wrap, 4 * i)
                    k = B[0][:, :].rearrange("p (h d) -> p h d", h=HKV)
                    cos = tabk[:, 0, :].unsqueeze(1).to_broadcast([P, HKV, HD])
                    nc.vector.tensor_tensor(kmul[:, b, 0], k, cos, ALU.mult)
                    sin = tabk[:, 1, 1:HD].unsqueeze(1).to_broadcast([P, HKV, HD - 1])
                    nc.vector.tensor_tensor(kmul[:, b, 1, :, 1:HD], k[:, :, 0:HD - 1], sin, ALU.mult)
                    sin0 = tabk[:, 1, 0:1].unsqueeze(1).to_broadcast([P, HKV, 1])
                    nc.vector.tensor_tensor(kmul[:, b, 1, :, 0:1], k[:, :, HD - 1:HD], sin0, ALU.mult).then_inc(k_mul, 1)

                def rotate_q(h):
                    kv, r = h // REP, h % REP
                    dve.wait_ge(q_proj, 16 * i + h + 1)
                    if r == 0:
                        if kv >= 2:
                            dve.wait_ge(s_mm, 8 * i + 2 * (kv - 1))
                        else:
                            dve.wait_ge(s_mm, 8 * i)
                    q = B[h % 2][:, :].rearrange("p (b l) -> p b l", l=L)
                    for c in range(2):
                        table = tabq[:, c, :].unsqueeze(1).to_broadcast([P, GN // L, L])
                        ins = nc.vector.tensor_tensor(qCS[:, kv % 2, c, r].rearrange("p (b l) -> p b l", l=L), q, table, ALU.mult)
                    ins.then_inc(q_rope, 1)

                def subtract_max(kv):
                    for u in range(2):
                        n = 8 * i + 2 * kv + u
                        s = B[4 + u][:, :].rearrange("p (g k) -> p g k", k=L)
                        dve.wait_ge(s_tr, n + 1)
                        nc.vector.tensor_reduce(out=sm[:, u, 0, :].unsqueeze(2), in_=s, axis=AX.X, op=ALU.max).then_inc(s_max, 1)
                        dve.wait_ge(s_max, n + 1)
                        if kv >= 1:
                            dve.wait_ge(p_ok, n - 1)
                        else:
                            dve.wait_ge(p_ok, 8 * i)
                        nc.vector.tensor_tensor(pr[:, u].rearrange("p (g k) -> p g k", k=L), s,
                                                sm[:, u, 0, :].unsqueeze(2).to_broadcast([P, 8, L]), ALU.subtract).then_inc(s_sub, 1)

                def row_sums(kv):
                    for u in range(2):
                        n = 8 * i + 2 * kv + u
                        dve.wait_ge(s_exp, n + 1)
                        nc.vector.tensor_reduce(out=sm[:, u, 1, :].unsqueeze(2), in_=pr[:, u].rearrange("p (g k) -> p g k", k=L),
                                                axis=AX.X, op=ALU.add).then_inc(s_sum, 1)
                        dve.wait_ge(s_sum, n + 1)
                        nc.vector.reciprocal(sm[:, u, 2, :], sm[:, u, 1, :]).then_inc(s_rec, 1)

                def out_lo(kv):
                    for p in range(GT):
                        dve.wait_ge(a_hi, 16 * i + 4 * kv + p + 1)
                        nc.vector.tensor_tensor(head_cols(aTl, kv, p), pv_cols(B[6 + p % 2]), head_cols(aTh, kv, p), ALU.subtract).then_inc(a_lo, 1)

                for j in range(GT):
                    multiply_k(j)
                for h in range(REP):
                    rotate_q(h)
                for kv in range(1, HKV):
                    rotate_q(REP * kv)
                    rotate_q(REP * kv + 1)
                    subtract_max(kv - 1)
                    rotate_q(REP * kv + 2)
                    rotate_q(REP * kv + 3)
                    row_sums(kv - 1)
                    out_lo(kv - 1)
                subtract_max(HKV - 1)
                if not last:
                    ln_statistics(nc, dve, tiles(i + 1), mv, stats, ln_st, ln_mv, i + 1, SETUP)
                row_sums(HKV - 1)
                if not last:
                    dve.wait_ge(xtr, 2 * i + 2)
                    normalise(i + 1)
                out_lo(HKV - 1)
                if not last:
                    xT_lo_parts(2 * i + 2)
                for j in range(GT):
                    dve.wait_ge(wo, 4 * i + j + 1)
                    xj = X[:, bass.ds(GT * i + j, 1), :].rearrange("p o d -> p (o d)")
                    nc.vector.scalar_tensor_tensor(xj, B[j][:, 0:D], 1.0 / (S_V * S_VO), xj, ALU.mult, ALU.add).then_inc(x_new, 1)

            in_loop(dve, body)

        @block.tensor
        def _(pe):
            def transpose_xhat(base):
                for j in range(GT):
                    pe.wait_ge(xhat_ok, 4 * base + j + 1)
                    for kt in range(KT):
                        ins = nc.tensor.transpose(B[6 + kt][:, j * P:(j + 1) * P], xhat[:, j, kt * P:(kt + 1) * P], ident[:, :])
                        if j == GT - 1:
                            ins.then_inc(xtr, 1)

            def w(c, lo, n, kt=0):
                cols = slice(kt * 512 + lo, kt * 512 + lo + n)
                return (WH[:, c, cols], WL[:, c, cols])

            pe.wait_ge(tab_in, 48)
            transpose_xhat(0)

            def body(i, last):
                def project_tokens(j, c, bank, done):
                    for kt in range(KT):
                        x = (xTh[:, kt, j * P:(j + 1) * P], xTl[:, kt, j * P:(j + 1) * P])
                        ins = matmul3(nc, bank[:, :], x, w(c, 0, 512, kt), kt == 0, kt == KT - 1)
                    ins.then_inc(done, 1)

                def project_kv(j):
                    if j >= 1:
                        pe.wait_ge(k_mul, 4 * i + j)
                    project_tokens(j, 0, B[0], k_proj)
                    if j >= 1:
                        pe.wait_ge(v_ok, 4 * i + j)
                    project_tokens(j, 1, B[1], v_proj)

                def transpose_k(j):
                    pe.wait_ge(k_ext, 4 * i + j + 1)
                    if j >= 1:
                        pe.wait_ge(k_T, 8 * i + 2 * j)
                    else:
                        pe.wait_ge(p_T, 8 * i)
                    for b in range(2):
                        for kv in range(2):
                            for c in range(2):
                                o = (2 * kv + c) * P
                                ins = nc.tensor.transpose(B[4 + b][:, o:o + P], kext[:, j % 2, 2 * b + kv, c:c + HD], ident[:, :])
                        ins.then_inc(k_tr, 1)

                def project_q(h):
                    if h == 0:
                        pe.wait_ge(k_mul, 4 * i + 4)
                    elif h == 1:
                        pe.wait_ge(v_ok, 4 * i + 4)
                    else:
                        pe.wait_ge(q_rope, 16 * i + h - 1)
                    for kt in range(KT):
                        ins = matmul3(nc, B[h % 2][:, :], w(2 + h // REP, (h % REP) * HD, HD, kt), (xTh[:, kt], xTl[:, kt]), kt == 0, kt == KT - 1)
                    ins.then_inc(q_proj, 1)

                def scores(kv):
                    pe.wait_ge(q_rope, 16 * i + REP * kv + REP)
                    for u in range(2):
                        if kv == 0:
                            pe.wait_ge(k_T, 8 * i + 4 * u + 4)
                        else:
                            pe.wait_ge(s_copy, 8 * i + 2 * kv + u - 1)
                        for pp in range(2):
                            p = 2 * u + pp
                            for c in range(2):
                                for s in range(2):
                                    rows = slice(64 * s, 64 * s + 64)
                                    ins = nc.tensor.matmul(B[2 + u][rows, pp * 256:(pp + 1) * 256], kT[:, p, kv, c, rows],
                                                           qCS[:, kv % 2, c, :, p * P + 64 * s:p * P + 64 * s + 64], start=c == 0, stop=c == 1)
                        ins.then_inc(s_mm, 1)

                def transpose_scores(kv):
                    for u in range(2):
                        n = 8 * i + 2 * kv + u
                        pe.wait_ge(s_copy, n + 1)
                        if kv == 0:
                            pe.wait_ge(k_T, 8 * i + 8)
                        else:
                            pe.wait_ge(p_T, n - 1)
                        for b in range(4):
                            ins = nc.tensor.transpose(B[4 + u][:, b * P:(b + 1) * P], st[:, u, b * P:(b + 1) * P], ident[:, :])
                        ins.then_inc(s_tr, 1)

                def transpose_probs(kv):
                    for u in range(2):
                        pe.wait_ge(p_ok, 8 * i + 2 * kv + u + 1)
                        for b in range(4):
                            ins = nc.tensor.transpose(B[4 + u][:, b * P:(b + 1) * P], pn[:, u, b * P:(b + 1) * P], ident[:, :])
                        ins.then_inc(p_tr, 1)

                def values(kv):
                    for p in range(GT):
                        n = 16 * i + 4 * kv + p
                        pe.wait_ge(p_T, 8 * i + 2 * kv + p // 2 + 1)
                        if 4 * kv + p >= 2:
                            pe.wait_ge(a_lo, n - 1)
                        else:
                            pe.wait_ge(a_lo, 16 * i)
                        for s in range(2):
                            ins = nc.tensor.matmul(B[6 + p % 2][:, s * 256:(s + 1) * 256], V[:, s, p, kv * HD:(kv + 1) * HD],
                                                   pT[:, p // 2, (p % 2) * 256:(p % 2 + 1) * 256], start=True, stop=True)
                        ins.then_inc(pv, 1)

                def project_out(j, h0, h1):
                    if h0 == 0:
                        if j < 2:
                            pe.wait_ge(q_rope, 16 * i + 15 + j)
                        else:
                            pe.wait_ge(s_copy, 8 * i + 5 + j)
                    for h in range(h0, h1):
                        if h % REP == 0:
                            pe.wait_ge(a_lo, 16 * i + h + j + 1)
                        stat = (aTh[:, h, j * P:(j + 1) * P], aTl[:, h, j * P:(j + 1) * P])
                        ins = matmul3(nc, B[j][:, 0:D], stat, wo_cols(h), h == 0, h == H - 1)
                    if h1 == H:
                        ins.then_inc(wo, 1)

                def wo_cols(h):
                    c, o = 6 + h // 4, (h % 4) * D
                    return (WH[:, c, o:o + D], WL[:, c, o:o + D])

                pe.wait_ge(xT_lo, 2 * i + 2)
                pe.wait_ge(x_new, 4 * i)
                pe.wait_ge(w_lo, 2)
                for j in range(3):
                    project_kv(j)
                transpose_k(0)
                project_kv(3)
                transpose_k(1)
                pe.wait_ge(w_lo, NCH)
                project_q(0)
                project_q(1)
                transpose_k(2)
                project_q(2)
                project_q(3)
                transpose_k(3)
                scores(0)
                for kv in range(1, HKV):
                    project_q(REP * kv)
                    project_q(REP * kv + 1)
                    transpose_scores(kv - 1)
                    project_q(REP * kv + 2)
                    project_q(REP * kv + 3)
                    transpose_probs(kv - 1)
                    scores(kv)
                    values(kv - 1)
                done = H - REP
                transpose_scores(HKV - 1)
                project_out(0, 0, done)
                transpose_probs(HKV - 1)
                project_out(1, 0, done)
                values(HKV - 1)
                if not last:
                    pe.wait_ge(a_lo, 16 * i + 16)
                    transpose_xhat(i + 1)
                project_out(0, done, H)
                project_out(1, done, H)
                project_out(2, 0, H)
                project_out(3, 0, H)

            in_loop(pe, body)


def block_b(nc, X, ident, WCh, WCl, a):
    with ExitStack() as ctx:
        def sb(name, shape, dt=F32):
            return ctx.enter_context(nc.sbuf_tensor("b_" + name, shape, dt))

        def sem(name):
            return ctx.enter_context(nc.semaphore("b_" + name))

        RING = 4
        Q = D
        y = sb("y", [P, 2, D])
        y32 = sb("y32", [P, 4, Q])
        c32 = sb("c32", [P, 4, Q])
        hm = sb("hm", [P, 2, 2 * Q], F16)
        yst = sb("yst", [P, RING, XS, Q], F16)
        kst = sb("kst", [P, 2, XS * Q], F16)
        kz = sb("kz", [P, RING, XJ, XS * Q], F16)
        vin = sb("vin", [P, 2, 2, 64])
        vst = sb("vst", [P, 2, 2, 2, XH, 32])
        pr = sb("pr", [P, 8, 512])
        mx = sb("mx", [P, 4, 8])
        mrow = sb("mrow", [XJ, 4, Q], F16)
        num = sb("num", [P, 2, 512])
        rec = sb("rec", [P, 2, 2, XJ])
        ret = sb("ret", [P, 2, 2, 64])
        gamma = sb("gamma", [P, 1])
        mask = sb("mask", [P, 2])
        stats = sb("stats", [P, 1, 6])
        mv = sb("mv", [P, 1, 2])
        rstd = sb("rstd", [P, 1])
        half = sb("half", [P, 1])
        wst = sb("wst", [P, CH])
        B = [ctx.enter_context(nc.psum_tensor(f"b_bank{n}", [P, 512], F32)) for n in range(8)]

        cst_in, zeroed, kz_zero, pool_init = sem("cst_in"), sem("zeroed"), sem("kz_zero"), sem("pool_init")
        ln_st, ln_mv, ln_add, ln_rs, y_ok = (sem(n) for n in ("ln_st", "ln_mv", "ln_add", "ln_rs", "y_ok"))
        y_out, y_in, c_in, v_in = sem("y_out"), sem("y_in"), sem("c_in"), sem("v_in")
        hm_y, y_cv, hm_k, k_cv, v_cv = sem("hm_y"), sem("y_cv"), sem("hm_k"), sem("k_cv"), sem("v_cv")
        kz_in = [sem(f"kz_in{n}") for n in range(RING)]
        m_mm, m_red, m_tr, m_row = sem("m_mm"), sem("m_red"), sem("m_tr"), sem("m_row")
        m_in = [sem(f"m_in{n}") for n in range(4)]
        e_mm, e_exp, pv, pv_ok = sem("e_mm"), sem("e_exp"), sem("pv"), sem("pv_ok")
        n_tr, n_rec, r_ok, r_tr, x_new = sem("n_tr"), sem("n_rec"), sem("r_ok"), sem("r_tr"), sem("x_new")
        c_sc, w_in, w_sc, w_hi, w_lo = sem("c_sc"), sem("w_in"), sem("w_sc"), sem("w_hi"), sem("w_lo")

        block = ctx.enter_context(nc.Block())
        SETUP = (cst_in, 32)
        PAIRS = TILES
        UN = 8
        ROUNDS = SEQS * XS // UN
        AHEAD = 3
        DMAS_Y, DMAS_K = XJ, XJ

        def in_loop(eng, body):
            body(0, True, 2)
            with eng.Fori(1, ROUNDS - 2) as i:
                body(i, False, 2)
            body(ROUNDS - 2, False, 1)
            body(ROUNDS - 1, False, 0)

        def max_comes(t, first, last):
            return not (first and t == 0) and not (last and t - 1 + AHEAD >= UN)

        def xtile(p):
            return X[:, bass.ds(p, 1), :].rearrange("p o d -> p (o d)")

        y_dram = nc.dram_tensor("y_rows", (2, XJ * XD, 2 * XS, D), F32, kind="Internal").ap()

        @block.sync
        def _(sp):
            def load_ctx(p):
                sp.wait_ge(k_cv, 2 * p)
                sp.dma_start(c32[:, :, :], a["ctxS"][bass.ds(p, 1)].rearrange("o p s q -> (o p) s q")).then_inc(c_in, 16)

            def load_values(p):
                sp.wait_ge(v_cv, p)
                sp.dma_start(vin[:, :, :, :], a["ctxT"][bass.ds(p, 1)].rearrange("o p (t b c) -> (o p) t b c", t=2, b=2)).then_inc(v_in, 16)

            def store_y(p, par):
                in_dram = [] if isinstance(p, int) and p < 2 else [(y_in, 16 * DMAS_Y * (p - 1))]
                wait_apart(sp, SETUP, (y_ok, p + 1), *in_dram)
                sp.dma_start(y_dram[par].rearrange("r s q -> s r q"), y[:, par, :]).then_inc(y_out, 16)

            def stack_y(p, par):
                sp.wait_ge(y_out, 16 * (p + 1))
                sp.wait_ge(y_cv, 2 * p)
                rows = y_dram[par].rearrange("(j d) s q -> j d (s q)", j=XJ)
                for j in range(XJ):
                    three = rows[j].unsqueeze(0).to_broadcast([3, XD, 4 * Q])
                    sp.dma_start(y32[32 * j:32 * j + 3 * XD, :, :].rearrange("p s q -> p (s q)"), three).then_inc(y_in, 16)

            def spread_k(b, r, *waits):
                wait_apart(sp, SETUP, (k_cv, b + 1), *waits)
                for j in range(XJ):
                    rows = slice(32 * j, 32 * j + 32)
                    sp.dma_start(kz[rows, r, j, :], kst[rows, r % 2, :]).then_inc(kz_in[r], 16)

            sp.dma_start(gamma[:, :], a["gamma"].to_broadcast([P, 1])).then_inc(cst_in, 16)
            sp.dma_start(mask[:, :], a["maskB"]).then_inc(cst_in, 16)
            for p in range(2):
                load_ctx(p)
                store_y(p, p)
                if p == 0:
                    sp.wait_ge(zeroed, 1)
                stack_y(p, p)
                if p == 0:
                    sp.wait_ge(kz_zero, 1)
                for q in range(2):
                    spread_k(2 * p + q, 2 * p + q)
                load_values(p)
            load_ctx(2)
            store_y(2, 0)

            def body(i, first, left):
                last = left == 0
                for t in range(UN):
                    s, p, q = UN * i + t, 2 * i + t // 4, t // 4
                    if t % 4 == 0 and not last:
                        stack_y(p + 2, q)
                    if t % 4 == 0 and not (first and t == 0) and not (last and t == 4):
                        load_values(p + 1)
                    if t == 0 and not first and not last:
                        sp.wait_ge(w_lo, i)
                        sp.dma_start(wst[:, :], a["wC"][bass.ds(i - 1, 1)].rearrange("o p n -> (o p) n")).then_inc(w_in, 16)
                    if t % 4 == 3 and left > q:
                        load_ctx(p + 3)
                        store_y(p + 3, 1 - q)
                    if t % 2 == 1 and not last:
                        spread_k(4 * i + (t - 1) // 2 + RING, (t - 1) // 2, (e_mm, 4 * s + 4))

            in_loop(sp, body)

        @block.gpsimd
        def _(pool):
            def convert_y(b, q, r, *waits):
                src = y32[:, 2 * q:2 * q + 2, :].rearrange("p s q -> p (s q)")
                wait_apart(pool, SETUP, (y_in, 8 * DMAS_Y * (b - q + 2)), (y_cv, b), *waits)
                nc.gpsimd.tensor_scalar(hm[:, 0], src, mask[:, 0:1], 1.0, ALU.mult, ALU.mult).then_inc(hm_y, 1)
                pool.wait_ge(hm_y, b + 1)
                nc.gpsimd.tensor_tensor(yst[:, r].rearrange("p s q -> p (s q)"), src, hm[:, 0], ALU.subtract).then_inc(y_cv, 1)

            def convert_k(b, q, *waits):
                src = c32[:, 2 * q:2 * q + 2, :].rearrange("p s q -> p (s q)")
                wait_apart(pool, SETUP, (c_in, 8 * (b - q + 2)))
                nc.gpsimd.tensor_scalar(src, src, S_C, 1.0, ALU.mult, ALU.mult).then_inc(c_sc, 1)
                wait_apart(pool, SETUP, (c_sc, b + 1), (k_cv, b))
                nc.gpsimd.tensor_scalar(hm[:, 1], src, mask[:, 1:2], 1.0, ALU.mult, ALU.mult).then_inc(hm_k, 1)
                pool.wait_ge(hm_k, b + 1)
                for sem, count in waits:
                    pool.wait_ge(sem, count)
                nc.gpsimd.tensor_tensor(kst[:, q, :], src, hm[:, 1], ALU.subtract).then_inc(k_cv, 1)

            def convert_v(p, par, *waits):
                wait_apart(pool, SETUP, (v_in, 16 * (p + 1)), *waits)
                nc.gpsimd.tensor_scalar(vst[:, par].rearrange("p t b h e -> p (t b h) e")[:, :, 0:XD],
                                        vin[:, :, :, :].rearrange("p t b (h d) -> p (t b h) d", d=XD),
                                        1.0, 0.0, ALU.mult, ALU.add).then_inc(v_cv, 1)

            def rstd_of(p):
                ln_rstd(nc, pool, mv, rstd, half[:, :], ln_mv, p + 1, ln_add, p + 1, ln_rs, SETUP, S_Y, [(y_ok, p)])

            nc.gpsimd.memset(half[:, :], -0.5).then_inc(pool_init, 1)
            nc.gpsimd.memset(wst[:, 0:1], 0.0).then_inc(w_lo, 1)
            pool.wait_ge(pool_init, 1)
            pool.wait_ge(cst_in, 32)
            rstd_of(0)
            nc.gpsimd.memset(y32[:, :, :], 0.0).then_inc(zeroed, 1)
            nc.gpsimd.memset(vst[:, :, :, :, :, :], 0.0).then_inc(pool_init, 1)
            for p in range(2):
                if p == 1:
                    rstd_of(1)
                for q in range(2):
                    convert_k(2 * p + q, q, *([(kz_in[q], 16 * DMAS_K)] if p == 1 else []))
                if p == 0:
                    pool.wait_ge(pool_init, 2)
                    nc.gpsimd.memset(vst[:, :, :, :, :, XD:XD + 1].rearrange("p a t b h e -> p (a t b h) e"), 1.0).then_inc(pool_init, 1)
                for q in range(2):
                    convert_y(2 * p + q, q, 2 * p + q)
            rstd_of(2)
            pool.wait_ge(pool_init, 3)
            convert_v(0, 0)

            def body(i, first, left):
                last = left == 0
                for q in range(2):
                    p, s0 = 2 * i + q, UN * i + 4 * q

                    def kst_spread(e):
                        r = 2 * q + 2 + e
                        return kz_in[r % RING], 16 * DMAS_K * (i + r // RING + 1)

                    chunk = bass.ds(i - 1, 1)
                    if not last:
                        convert_k(2 * p + 4, 0, kst_spread(0))
                    if not last:
                        convert_y(2 * p + 4, 0, 2 * q, (e_mm, 4 * (s0 + 2)))
                    if left > q:
                        rstd_of(p + 3)
                    if not last:
                        convert_k(2 * p + 5, 1, kst_spread(1))
                    if not (last and q == 1):
                        convert_v(p + 1, (q + 1) % 2, *([] if first and q == 0 else [(pv, s0)]))
                    if q == 0 and not first and not last:
                        wait_apart(pool, SETUP, (w_in, 16 * i))
                        nc.gpsimd.tensor_scalar(wst[:, :], wst[:, :], S_W, 1.0, ALU.mult, ALU.mult).then_inc(w_sc, 1)
                    if q == 1 and not first and not last:
                        pool.wait_ge(w_hi, i)
                        hi = WCh[:, chunk, :].rearrange("p o n -> p (o n)")
                        nc.gpsimd.tensor_tensor(WCl[:, chunk, :].rearrange("p o n -> p (o n)"), wst[:, :], hi, ALU.subtract).then_inc(w_lo, 1)
                    if not last:
                        convert_y(2 * p + 5, 1, 2 * q + 1, (e_mm, 4 * (s0 + 4)))

            in_loop(pool, body)

        @block.scalar
        def _(act):
            def copy_max(s, t):
                act.wait_ge(m_tr, s + 1)
                if not (isinstance(s, int) and s < 4):
                    act.wait_ge(m_in[t % 4], 4 * (s - t % 4))
                nc.scalar.activation(mrow[:, t % 4, :], B[7][0:XJ, 0:Q], ACT.Copy, scale=-1.0 / (S_Y * S_C)).then_inc(m_row, 1)

            def insert_max(s, t):
                act.wait_ge(m_row, s + 1)
                act.dma_start(yst[MAXROW:P:32, t // 2 % RING, t % 2, :], mrow[:, t % 4, :]).then_inc(m_in[t % 4], 16)

            def copy_numerators(b, par):
                act.wait_ge(pv, 2 * b + 2)
                if not (isinstance(b, int) and b < 2):
                    act.wait_ge(n_tr, b - 1)
                nc.scalar.activation(num[:, par, :], B[6][:, :], ACT.Copy).then_inc(pv_ok, 1)

            for s in range(AHEAD):
                copy_max(s, s)
                insert_max(s, s)

            def body(i, first, left):
                last = left == 0
                for t in range(UN):
                    s = UN * i + t
                    for k in range(XJ):
                        act.wait_ge(e_mm, 4 * s + k + 1)
                        if k == 0 and not (first and t < 2):
                            act.wait_ge(pv, s - 1)
                        nc.scalar.activation(pr[:, 4 * (t % 2) + k, :], B[2 + k][:, :], ACT.Exp,
                                             scale=1.0 / (S_Y * S_C * float(np.sqrt(XD)))).then_inc(e_exp, 1)
                        if k == 0 and max_comes(t, first, last):
                            copy_max(s - 1 + AHEAD, (t - 1 + AHEAD) % UN)
                        if k == 1 and max_comes(t, first, last):
                            insert_max(s - 1 + AHEAD, (t - 1 + AHEAD) % UN)
                    if t % 2 == 0 and not (first and t == 0):
                        copy_numerators(4 * i + t // 2 - 1, (t // 2 - 1) % 2)
                    if t == 5 and not first and not last:
                        act.wait_ge(w_sc, i)
                        nc.scalar.activation(WCh[:, bass.ds(i - 1, 1), :].rearrange("p o n -> p (o n)"), wst[:, :], ACT.Copy).then_inc(w_hi, 1)

            in_loop(act, body)
            copy_numerators(SEQS - 1, 1)

        @block.vector
        def _(dve):
            def statistics(p):
                ln_statistics(nc, dve, [xtile(p)], mv, stats, ln_st, ln_mv, p, SETUP)

            def normalise(p, par):
                dve.wait_ge(ln_rs, p + 1)
                if not (isinstance(p, int) and p < 2):
                    dve.wait_ge(y_out, 16 * (p - 1))
                ln_normalise(nc, dve, xtile(p), y[:, par, :], mv, rstd, 0, y_ok)

            def reduce_max(s, t, k):
                dve.wait_ge(m_mm, 4 * s + k + 1)
                if k == 0 and not (isinstance(s, int) and s < 4):
                    dve.wait_ge(m_tr, s - 3)
                nc.vector.tensor_reduce(out=mx[:, t % 4, k::XJ].unsqueeze(2), in_=B[k % 2][:, :].rearrange("p (t l) -> p t l", t=2),
                                        axis=AX.X, op=ALU.max).then_inc(m_red, 1)

            def divide(b, q, pair):
                dve.wait_ge(n_tr, b + 1)
                v = B[7][:, :].rearrange("p (h t j r) -> p h t j r", h=2, t=2, j=XJ)
                nc.vector.reciprocal(rec[:, :, :, :].unsqueeze(4), v[:, :, :, :, XD:XD + 1]).then_inc(n_rec, 1)
                dve.wait_ge(n_rec, b + 1)
                if q == 0:
                    dve.wait_ge(r_tr, pair)
                for t in range(2):
                    ins = nc.vector.tensor_tensor(ret[:, t, q, :].rearrange("p (h j d) -> p h j d", h=2, j=XJ), v[:, :, t, :, 0:XD],
                                                  rec[:, :, t, :].unsqueeze(3).to_broadcast([P, 2, XJ, XD]), ALU.mult)
                ins.then_inc(r_ok, 1)

            def add_output(p):
                dve.wait_ge(r_tr, p + 1)
                nc.vector.scalar_tensor_tensor(xtile(p), B[7][:, 0:D], gamma[:, 0:1], xtile(p), ALU.mult, ALU.add).then_inc(x_new, 1)

            for p in range(3):
                statistics(p)
                if p == 0:
                    nc.vector.memset(kz[:, :, :, :], 0.0).then_inc(kz_zero, 1)
                normalise(p, p % 2)
            for s in range(AHEAD):
                for k in range(XJ):
                    reduce_max(s, s, k)
            dve.wait_ge(cst_in, 32)

            def body(i, first, left):
                last = left == 0
                for t in range(UN):
                    s = UN * i + t
                    more = not (last and t + AHEAD >= UN)
                    for k in range(XJ):
                        if more:
                            reduce_max(s + AHEAD, (t + AHEAD) % UN, k)
                        if k == 0 and t % 4 == 2 and left > t // 4:
                            statistics(2 * i + t // 4 + 3)
                        if k == 3 and t % 2 == 1 and not (first and t < 3):
                            b = 4 * i + (t - 3) // 2
                            divide(b, ((t - 3) // 2) % 2, 2 * i + (t - 3) // 4)
                        if k == 3 and t % 4 == 2 and not (first and t < 6):
                            add_output(2 * i + (t - 6) // 4)
                    if t % 4 == 3 and left > t // 4:
                        normalise(2 * i + t // 4 + 3, 1 - t // 4)

            in_loop(dve, body)
            divide(SEQS - 1, 1, PAIRS - 1)
            add_output(PAIRS - 1)

        @block.tensor
        def _(pe):
            def maxima_scores(i, t, k):
                r, h, g = t // 2 % RING, t % 2, 4 * (UN * i + t) + k
                if k == 0 and t % 2 == 0:
                    pe.wait_ge(y_cv, 4 * i + t // 2 + 1)
                    pe.wait_ge(kz_in[r], 16 * DMAS_K * (i + t // UN + 1))
                if not (isinstance(g, int) and g < 2):
                    pe.wait_ge(m_red, g - 1)
                for q in range(2):
                    ins = nc.tensor.matmul(B[k % 2][:, q * Q:(q + 1) * Q], yst[:, r, h, q * P:(q + 1) * P],
                                           kz[:, r, k, h * Q:(h + 1) * Q], start=True, stop=True)
                ins.then_inc(m_mm, 1)

            def scores(s, t, k):
                r, h, g = t // 2, t % 2, 4 * s + k
                if k == 0:
                    pe.wait_ge(m_in[t % 4], 4 * (s - t % 4) + 16)
                if not (isinstance(g, int) and g < 4):
                    pe.wait_ge(e_exp, g - 3)
                for l in range(2):
                    ins = nc.tensor.matmul(B[2 + k][:, l * Q:(l + 1) * Q], kz[:, r, k, h * Q + l * P:h * Q + (l + 1) * P],
                                           yst[:, r, h, :], start=True, stop=True)
                ins.then_inc(e_mm, 1)

            def products(i, t):
                b, h, par = t // 2 % 2, t % 2, t // 4 % 2
                pe.wait_ge(e_exp, 4 * (UN * i + t) + 4)
                if t % 4 == 0:
                    pe.wait_ge(v_cv, 2 * i + t // 4 + 1)
                if h == 0:
                    pe.wait_ge(pv_ok, 4 * i + t // 2)
                for l in range(2):
                    for j in range(XJ):
                        ins = nc.tensor.matmul(B[6][32 * j:32 * j + 32, h * Q:(h + 1) * Q], vst[:, par, l, b, XJ * h + j, :],
                                               pr[:, 4 * (t % 2) + j, l * Q:(l + 1) * Q], start=l == 0, stop=l == 1)
                ins.then_inc(pv, 1)

            def transpose_max(s, t):
                pe.wait_ge(m_red, 4 * s + 4)
                for q in range(2):
                    ins = nc.tensor.transpose(B[7][0:XJ, q * P:(q + 1) * P], mx[:, t % 4, XJ * q:XJ * q + XJ], ident[:, :])
                ins.then_inc(m_tr, 1)

            def transpose_numerators(b, par):
                pe.wait_ge(pv_ok, b + 1)
                for h in range(2):
                    for t in range(2):
                        o = (2 * h + t) * P
                        ins = nc.tensor.transpose(B[7][:, o:o + P], num[:, par, h * Q + t * P:h * Q + (t + 1) * P], ident[:, :])
                ins.then_inc(n_tr, 1)

            def transpose_output(p):
                pe.wait_ge(r_ok, 2 * p + 2)
                for t in range(2):
                    ins = nc.tensor.transpose(B[7][:, t * P:(t + 1) * P], ret[:, t].rearrange("p b c -> p (b c)"), ident[:, :])
                ins.then_inc(r_tr, 1)

            for s in range(AHEAD):
                for k in range(XJ):
                    maxima_scores(0, s, k)
                if s >= 1:
                    pe.wait_ge(m_row, s)
                transpose_max(s, s)

            def body(i, first, left):
                last = left == 0
                for t in range(UN):
                    s = UN * i + t
                    more = not (last and t + AHEAD >= UN)
                    divides = t % 2 == 1 and not (first and t < 3)
                    outputs = t % 4 == 2 and not (first and t < 6)
                    for k in range(XJ):
                        if more:
                            maxima_scores(i, t + AHEAD, k)
                        scores(s, t, k)
                        if k == 0 and max_comes(t, first, last):
                            if t % 2 == 0 and not (first and t < 4):
                                pe.wait_ge(r_ok, 4 * i + t // 2 - 1)
                            elif t % 4 == 3 and not (first and t < 7):
                                pe.wait_ge(x_new, 2 * i + (t - 7) // 4 + 1)
                            else:
                                pe.wait_ge(m_row, s - 1 + AHEAD)
                            transpose_max(s - 1 + AHEAD, (t - 1 + AHEAD) % UN)
                        if k == 2 and (divides or outputs):
                            if not last or t <= UN - AHEAD:
                                pe.wait_ge(m_row, s + AHEAD)
                            if divides:
                                if last and t > UN - AHEAD:
                                    pe.wait_ge(x_new, 2 * i + 1)
                                transpose_numerators(4 * i + (t - 3) // 2, ((t - 3) // 2) % 2)
                            else:
                                if last and t > UN - AHEAD:
                                    pe.wait_ge(r_ok, 4 * i + 2)
                                transpose_output(2 * i + (t - 6) // 4)
                    if not (first and t == 0):
                        products(i if t else i - 1, (t - 1) % UN)

            in_loop(pe, body)
            products(ROUNDS - 1, UN - 1)
            pe.wait_ge(r_ok, SEQS - 1)
            transpose_numerators(SEQS - 1, 1)
            transpose_output(PAIRS - 1)


def block_c(nc, X, ident, WCh, WCl, a, out):
    with ExitStack() as ctx:
        def sb(name, shape, dt=F32):
            return ctx.enter_context(nc.sbuf_tensor("c_" + name, shape, dt))

        def sem(name):
            return ctx.enter_context(nc.semaphore("c_" + name))

        NG = E + 1
        LO = 32
        zhat = sb("zhat", [P, GT, D])
        stats = sb("stats", [P, GT, 6])
        mv = sb("mv", [P, GT, 2])
        rstd = sb("rstd", [P, GT])
        half = sb("half", [P, GT])
        zTh = sb("zth", [P, KT, GN], F16)
        zTl = sb("ztl", [P, KT, GN], F16)
        hTh = sb("hth", [P, MT, GN], F16)
        hTl = sb("htl", [P, MT, GN], F16)
        th = sb("th", [P, 2, GN])
        gs = sb("gs", [P, 2, GN])
        gu = sb("gu", [P, 2, GN])
        hs = sb("hs", [P, 2, GN])
        lg = sb("lg", [P, GT, NG])
        before = sb("before", [P, E, E])
        above = sb("above", [P, GT, E, E])
        ties = sb("ties", [P, GT, E, E])
        rank = sb("rank", [P, GT, E])
        top = sb("top", [P, GT])
        ex = sb("ex", [P, GT, E])
        gate = sb("gate", [P, GT, 1])
        den = sb("den", [P, 2, GT])
        cmb = sb("cmb", [P, GT, 2, LO])
        cT = sb("ct", [P, GN], F16)
        sel = sb("sel", [P, HID], F16)
        B = [ctx.enter_context(nc.psum_tensor(f"c_bank{n}", [P, 512], F32)) for n in range(8)]

        cst_in, init = sem("cst_in"), sem("init")
        ln_st, ln_mv, ln_add, ln_rs, z_ok, z_tr = (sem(n) for n in ("ln_st", "ln_mv", "ln_add", "ln_rs", "z_ok", "z_tr"))
        zT_hi, zT_lo = sem("zt_hi"), sem("zt_lo")
        g_mm, u_mm, c_mm = sem("g_mm"), sem("u_mm"), sem("c_mm")
        th_ok, gs_ok, gu_ok, hs_ok, h_hi, h_lo = (sem(n) for n in ("th_ok", "gs_ok", "gu_ok", "hs_ok", "h_hi", "h_lo"))
        dn, x_new, stored = sem("dn"), sem("x_new"), sem("stored")
        rt_mm, lg_ok, route, ex_ok, gate_ok, cmb_ok = (sem(n) for n in ("rt_mm", "lg_ok", "route", "ex_ok", "gate_ok", "cmb_ok"))
        rel_ok = sem("rel_ok")
        c_tr, cT_hi, cT_lo = sem("c_tr"), sem("ct_hi"), sem("ct_lo")

        block = ctx.enter_context(nc.Block())
        SETUP = (init, 3)
        LAST = GROUPS - 1
        NR = 9

        def in_loop(eng, body):
            body(0, False)
            with eng.Fori(1, LAST) as i:
                body(i, False)
            body(LAST, True)

        def tiles(group):
            return [X[:, bass.ds(GT * group + j, 1), :].rearrange("p o d -> p (o d)") for j in range(GT)]

        def wcols(off, n):
            return tuple(w[:, :, :].rearrange("p c n -> p (c n)")[:, off:off + n] for w in (WCh, WCl))

        @block.sync
        def _(sp):
            sp.dma_start(sel[:, :], a["sel"]).then_inc(cst_in, 16)
            sp.dma_start(before[:, :, :], a["before"].rearrange("p (e f) -> p e f", e=E)).then_inc(cst_in, 16)

            def body(i, last):
                sp.wait_ge(x_new, GT * i + GT)
                og = out.rearrange("(g t p) d -> g p t d", p=P, t=GT)
                sp.dma_start(og[bass.ds(i, 1)].rearrange("o p t d -> (o p) t d"), X[:, bass.ds(GT * i, GT), :]).then_inc(stored, 16)

            in_loop(sp, body)
            sp.wait_ge(stored, 16 * GROUPS)

        @block.gpsimd
        def _(pool):
            nc.gpsimd.memset(half[:, :], -0.5).then_inc(init, 1)
            nc.gpsimd.memset(cmb[:, :, :, :], 0.0).then_inc(init, 1)
            nc.gpsimd.memset(cT[:, :], 0.0).then_inc(init, 1)
            pool.wait_ge(init, 3)
            ln_rstd(nc, pool, mv, rstd, half[:, :], ln_mv, GT, ln_add, 1, ln_rs, SETUP)

            def body(i, last):
                for m in range(MT):
                    n = MT * i + m
                    pool.wait_ge(h_hi, n + 1)
                    if m == 0:
                        pool.wait_ge(dn, GT * i)
                    nc.gpsimd.tensor_tensor(hTl[:, m], hs[:, m % 2], hTh[:, m], ALU.subtract).then_inc(h_lo, 1)
                    if m == MT // 2 and not last:
                        used = (z_ok, GT * i + GT)
                        ln_rstd(nc, pool, mv, rstd, half[:, :], ln_mv, GT * i + 2 * GT, ln_add, i + 2, ln_rs, SETUP, waits=[used])

            in_loop(pool, body)

        @block.scalar
        def _(act):
            def zT_hi_parts(g):
                for kt in range(KT):
                    act.wait_ge(z_tr, KT * g + kt + 1)
                    nc.scalar.activation(zTh[:, kt], B[kt][:, :], ACT.Copy, scale=S_X).then_inc(zT_hi, 1)

            def route_exps(g):
                act.wait_ge(rel_ok, g + 1)
                nc.scalar.activation(ex[:, :, :], ex[:, :, :], ACT.Exp).then_inc(ex_ok, 1)
                nc.scalar.activation(gate[:, :, :], lg[:, :, E:NG], ACT.Tanh, scale=0.5).then_inc(gate_ok, 1)

            def cT_hi_part(g):
                act.wait_ge(c_tr, g + 1)
                nc.scalar.activation(cT[0:2 * LO, :], B[3][0:2 * LO, :], ACT.Copy, scale=S_CMB).then_inc(cT_hi, 1)

            zT_hi_parts(0)
            route_exps(0)
            act.wait_ge(init, 3)
            cT_hi_part(0)

            def body(i, last):
                def tanh(m):
                    n = MT * i + m
                    act.wait_ge(g_mm, n + 1)
                    if m >= 2:
                        act.wait_ge(gs_ok, n - 1)
                    nc.scalar.activation(th[:, m % 2], B[m % 2][:, :], ACT.Tanh, scale=0.5 / (S_X * S_W)).then_inc(th_ok, 1)

                def hidden_hi(m):
                    n = MT * i + m
                    if m == 0:
                        act.wait_ge(dn, GT * i)
                    act.wait_ge(hs_ok, n + 1)
                    nc.scalar.activation(hTh[:, m], hs[:, m % 2], ACT.Copy).then_inc(h_hi, 1)

                act.wait_ge(gs_ok, MT * i)
                tanh(0)
                for m in range(1, MT):
                    tanh(m)
                    hidden_hi(m - 1)
                hidden_hi(MT - 1)
                if not last:
                    zT_hi_parts(i + 1)
                    route_exps(i + 1)
                    cT_hi_part(i + 1)

            in_loop(act, body)

        @block.vector
        def _(dve):
            def normalise(g):
                dve.wait_ge(ln_rs, g + 1)
                for j, src in enumerate(tiles(g)):
                    ln_normalise(nc, dve, src, zhat[:, j, :], mv, rstd, j, z_ok)

            def zT_lo_parts(g):
                for kt in range(KT):
                    dve.wait_ge(zT_hi, KT * g + kt + 1)
                    nc.vector.scalar_tensor_tensor(zTl[:, kt], B[kt][:, :], S_X, zTh[:, kt], ALU.mult, ALU.subtract).then_inc(zT_lo, 1)

            def routing(g):
                dve.wait_ge(rt_mm, g + 1)
                nc.vector.tensor_scalar(lg[:, :, :], B[2][:, 0:GT * NG].rearrange("p (t e) -> p t e", e=NG),
                                        1.0 / (S_X * S_W), None, ALU.mult).then_inc(lg_ok, 1)
                dve.wait_ge(lg_ok, g + 1)
                l = lg[:, :, 0:E]
                nc.vector.tensor_reduce(out=top[:, :].unsqueeze(2), in_=l, axis=AX.X, op=ALU.max).then_inc(route, 1)
                dve.wait_ge(route, NR * g + 1)
                nc.vector.tensor_tensor(ex[:, :, :], l, top[:, :].unsqueeze(2).to_broadcast([P, GT, E]), ALU.subtract).then_inc(rel_ok, 1)
                one, two = l.unsqueeze(3).to_broadcast([P, GT, E, E]), l.unsqueeze(2).to_broadcast([P, GT, E, E])
                nc.vector.tensor_tensor(ties[:, :, :, :], two, one, ALU.is_equal).then_inc(route, 1)
                nc.vector.tensor_tensor(above[:, :, :, :], two, one, ALU.is_gt).then_inc(route, 1)
                dve.wait_ge(route, NR * g + 2)
                nc.vector.tensor_tensor(ties[:, :, :, :], ties[:, :, :, :], before[:, :, :].unsqueeze(1).to_broadcast([P, GT, E, E]),
                                        ALU.mult).then_inc(route, 1)
                dve.wait_ge(route, NR * g + 4)
                nc.vector.tensor_tensor(above[:, :, :, :], above[:, :, :, :], ties[:, :, :, :], ALU.add).then_inc(route, 1)
                dve.wait_ge(route, NR * g + 5)
                nc.vector.tensor_reduce(out=rank[:, :, :].unsqueeze(3), in_=above[:, :, :, :], axis=AX.X, op=ALU.add).then_inc(route, 1)
                dve.wait_ge(route, NR * g + 6)
                dve.wait_ge(ex_ok, g + 1)
                nc.vector.scalar_tensor_tensor(ex[:, :, :], rank[:, :, :], 2.0, ex[:, :, :], ALU.is_lt, ALU.mult).then_inc(route, 1)
                dve.wait_ge(route, NR * g + 7)
                nc.vector.tensor_reduce(out=den[:, 0, :].unsqueeze(2), in_=ex[:, :, :], axis=AX.X, op=ALU.add).then_inc(route, 1)
                dve.wait_ge(route, NR * g + 8)
                nc.vector.reciprocal(den[:, 1, :], den[:, 0, :]).then_inc(route, 1)
                dve.wait_ge(route, NR * g + 9)
                dve.wait_ge(c_tr, g)
                dve.wait_ge(gate_ok, g + 1)
                for copy in range(2):
                    nc.vector.tensor_tensor(cmb[:, :, copy, 0:E], ex[:, :, :], den[:, 1, :].unsqueeze(2).to_broadcast([P, GT, E]), ALU.mult)
                    ins = nc.vector.tensor_scalar(cmb[:, :, copy, E:NG], gate[:, :, :], 0.5, 0.5, ALU.mult, ALU.add)
                ins.then_inc(cmb_ok, 1)

            def cT_lo_part(g):
                dve.wait_ge(cT_hi, g + 1)
                lo = cT[LO:2 * LO, :]
                nc.vector.scalar_tensor_tensor(lo, B[3][LO:2 * LO, :], S_CMB, lo, ALU.mult, ALU.subtract).then_inc(cT_lo, 1)

            ln_statistics(nc, dve, tiles(0), mv, stats, ln_st, ln_mv, 0, SETUP)
            normalise(0)
            zT_lo_parts(0)
            dve.wait_ge(cst_in, 32)
            dve.wait_ge(init, 3)
            routing(0)
            cT_lo_part(0)

            def body(i, last):
                def hidden(m):
                    n, b = MT * i + m, m % 2
                    dve.wait_ge(th_ok, n + 1)
                    dve.wait_ge(gu_ok, n)
                    nc.vector.scalar_tensor_tensor(gs[:, b], th[:, b], 1.0, B[b][:, :], ALU.add, ALU.mult).then_inc(gs_ok, 1)
                    dve.wait_ge(gs_ok, n + 1)
                    dve.wait_ge(u_mm, n + 1)
                    nc.vector.tensor_tensor(gu[:, b], gs[:, b], B[2 + b][:, :], ALU.mult).then_inc(gu_ok, 1)
                    dve.wait_ge(gu_ok, n + 1)
                    dve.wait_ge(c_mm, n + 1)
                    if m >= 2:
                        dve.wait_ge(h_lo, n - 1)
                    else:
                        dve.wait_ge(h_lo, MT * i)
                    scale = 0.5 / (S_X * S_W) ** 2 * S_H / S_CMB
                    nc.vector.scalar_tensor_tensor(hs[:, b], gu[:, b], scale, B[4 + b][:, :], ALU.mult, ALU.mult).then_inc(hs_ok, 1)

                def add_output(j):
                    dve.wait_ge(dn, GT * i + j + 1)
                    xj = tiles(i)[j]
                    nc.vector.scalar_tensor_tensor(xj, B[6 + j % 2][:, 0:D], 1.0 / (S_H * S_W), xj, ALU.mult, ALU.add).then_inc(x_new, 1)

                for m in range(MT):
                    hidden(m)
                    if m == MT // 2 - 2 and not last:
                        ln_statistics(nc, dve, tiles(i + 1), mv, stats, ln_st, ln_mv, i + 1, SETUP)
                    if m == MT // 2 + 2 and not last:
                        normalise(i + 1)
                add_output(0)
                if not last:
                    zT_lo_parts(i + 1)
                add_output(1)
                if not last:
                    routing(i + 1)
                add_output(2)
                add_output(3)
                if not last:
                    cT_lo_part(i + 1)

            in_loop(dve, body)

        @block.tensor
        def _(pe):
            def transpose_z(g):
                for j in range(GT):
                    pe.wait_ge(z_ok, GT * g + j + 1)
                    for kt in range(KT):
                        ins = nc.tensor.transpose(B[kt][:, j * P:(j + 1) * P], zhat[:, j, kt * P:(kt + 1) * P], ident[:, :])
                        if j == GT - 1:
                            ins.then_inc(z_tr, 1)

            def router(g):
                pe.wait_ge(zT_lo, KT * g + KT)
                for j in range(GT):
                    for kt in range(KT):
                        z = (zTh[:, kt, j * P:(j + 1) * P], zTl[:, kt, j * P:(j + 1) * P])
                        ins = matmul3(nc, B[2][:, NG * j:NG * j + NG], z, wcols(RT_OFF + NG * kt, NG), kt == 0, kt == KT - 1)
                ins.then_inc(rt_mm, 1)

            def transpose_weights(g):
                wait_apart(pe, SETUP, (cmb_ok, g + 1))
                pe.wait_ge(*SETUP)
                for j in range(GT):
                    ins = nc.tensor.transpose(B[3][0:2 * LO, j * P:(j + 1) * P], cmb[:, j].rearrange("p a c -> p (a c)"), ident[:, :])
                ins.then_inc(c_tr, 1)

            transpose_z(0)
            router(0)
            transpose_weights(0)
            pe.wait_ge(cst_in, 32)

            def body(i, last):
                def gate_up(m):
                    n = MT * i + m
                    for bank, off, done, read in ((m % 2, 0, g_mm, gs_ok), (2 + m % 2, HID, u_mm, gu_ok)):
                        pe.wait_ge(read, n - 1 if m >= 2 else MT * i)
                        for kt in range(KT):
                            w = wcols(GU_OFF + kt * 2 * HID + off + m * P, P)
                            ins = matmul3(nc, B[bank][:, :], w, (zTh[:, kt], zTl[:, kt]), kt == 0, kt == KT - 1)
                        ins.then_inc(done, 1)
                    if m == 0:
                        pe.wait_ge(cT_lo, i + 1)
                    pe.wait_ge(hs_ok, n - 1 if m >= 2 else MT * i)
                    nc.tensor.matmul(B[4 + m % 2][:, :], sel[:, m * P:(m + 1) * P], cT[:, :], start=True, stop=True).then_inc(c_mm, 1)

                def down(j):
                    pe.wait_ge(x_new, GT * i + j - 1 if j >= 2 else GT * i)
                    for m in range(MT):
                        if j == 0:
                            pe.wait_ge(h_lo, MT * i + m + 1)
                        h = (hTh[:, m, j * P:(j + 1) * P], hTl[:, m, j * P:(j + 1) * P])
                        ins = matmul3(nc, B[6 + j % 2][:, 0:D], h, wcols(DN_OFF + m * D, D), m == 0, m == MT - 1)
                    ins.then_inc(dn, 1)

                pe.wait_ge(zT_lo, KT * i + KT)
                pe.wait_ge(lg_ok, i + 1)
                pe.wait_ge(cT_lo, i + 1)
                for m in range(MT):
                    gate_up(m)
                down(0)
                if not last:
                    pe.wait_ge(gs_ok, MT * i + MT)
                    transpose_z(i + 1)
                down(1)
                if not last:
                    pe.wait_ge(gu_ok, MT * i + MT)
                    router(i + 1)
                down(2)
                down(3)
                if not last:
                    transpose_weights(i + 1)

            in_loop(pe, body)


def build(nc, a, out, phases="ABC"):
    with ExitStack() as ctx:
        X = ctx.enter_context(nc.sbuf_tensor("x_res", [P, TILES, D], F32))
        ident = ctx.enter_context(nc.sbuf_tensor("ident", [P, P], F32))
        block_a(nc, X, ident, a)
        if "B" in phases:
            WCh = ctx.enter_context(nc.sbuf_tensor("wc_hi", [P, WC_CHUNKS, CH], F16))
            WCl = ctx.enter_context(nc.sbuf_tensor("wc_lo", [P, WC_CHUNKS, CH], F16))
            block_b(nc, X, ident, WCh, WCl, a)
        if "C" in phases:
            block_c(nc, X, ident, WCh, WCl, a, out)
        else:
            with nc.semaphore("dbg") as dbg, nc.Block() as block:
                @block.sync
                def _(sp):
                    sp.dma_start(out.rearrange("(t p) d -> p t d", p=P), X[:, :, :]).then_inc(dbg, 16)
                    sp.wait_ge(dbg, 16)


def rope_tables():
    inv = (np.float32(1.0) / np.float32(10000.0) ** (np.arange(0, HD, 2, dtype=np.float32) / np.float32(HD))).astype(np.float32)
    ang = np.arange(L, dtype=np.float32)[:, None] * inv[None, :]
    ang = np.concatenate([ang, ang], axis=-1).astype(np.float64)
    return np.cos(ang), np.sin(ang)


def constants():
    cos, sin = rope_tables()
    q = 1.0 / (S_X * S_W * np.sqrt(float(HD)))
    tabq = np.concatenate([cos.T * q, np.roll(sin, -1, axis=1).T * q], axis=1)
    k = 1.0 / (S_X * S_W)
    tabk = np.concatenate([np.tile(cos * k, (2, 1)), np.tile(sin * k, (2, 1))], axis=1)
    mask = np.zeros((P, 2), np.float32)
    r = np.arange(P) % 32
    mask[:, 0] = np.where((r >= XD) & (r < 2 * XD), 1, 0)
    mask[:, 1] = np.where((r >= 2 * XD) & (r < 3 * XD), 1, 0)
    sel = np.zeros((P, HID), np.float16)
    for n in range(E * I_MOE + I_SH):
        e = min(n // I_MOE, E)
        sel[e, n] = sel[32 + e, n] = 1
    before = np.tile(np.tril(np.ones((E, E), np.float32), -1).reshape(1, E * E), (P, 1))
    return {"maskB": mask, "sel": sel, "before": before, "tabq": tabq.astype(np.float32), "tabk": tabk.astype(np.float32), "ident": np.eye(P, dtype=np.float32)}


def layout(x, ctx_2048, L0_attn_Wq, L0_attn_Wk, L0_attn_Wv, L0_attn_Wo, L0_xattn_gamma, L0_ffn_router_weight,
           L0_ffn_gate_up_proj, L0_ffn_down_proj, L0_ffn_sh_gate_w, L0_ffn_sh_up_w, L0_ffn_sh_down_w, L0_ffn_shared_gate_w):
    arr = {"x": x.reshape(T, D)}

    def by_kt(w):
        return w.reshape(KT, P, -1).transpose(1, 0, 2).reshape(P, -1)

    chunks = [by_kt(L0_attn_Wk), by_kt(L0_attn_Wv)]
    chunks += [by_kt(L0_attn_Wq[:, c * 512:(c + 1) * 512]) for c in range(4)]
    wo = L0_attn_Wo.reshape(H, HD, D).transpose(1, 0, 2)
    chunks += [wo[:, 4 * c:4 * c + 4].reshape(P, CH) for c in range(4)]
    arr["wA"] = np.stack(chunks)
    c = ctx_2048.reshape(TILES, 2, XS, XJ, XD, D)
    st = np.zeros((TILES, XJ, 32, 2, XS, D), np.float32)
    for n in range(3):
        st[:, :, XD * n:XD * n + XD] = c.transpose(0, 3, 4, 1, 2, 5)
    st[:, :, MAXROW] = S_Y
    arr["ctxS"] = st.reshape(TILES, P, 2 * XS, D)
    arr["ctxT"] = ctx_2048.reshape(TILES, 2, 64, 2, P).transpose(0, 4, 3, 1, 2).reshape(TILES, P, 2 * 2 * 64)
    arr["gamma"] = L0_xattn_gamma.reshape(1, 1)
    gate = np.concatenate([L0_ffn_gate_up_proj[:, :I_MOE].reshape(-1, D), L0_ffn_sh_gate_w])
    up = np.concatenate([L0_ffn_gate_up_proj[:, I_MOE:].reshape(-1, D), L0_ffn_sh_up_w])
    down = np.concatenate([L0_ffn_down_proj.transpose(0, 2, 1).reshape(-1, D), L0_ffn_sh_down_w.T])
    pad = np.zeros((HID - gate.shape[0], D), np.float32)
    gu = np.concatenate([gate, pad, up, pad]).T
    dn = np.concatenate([down, pad]).reshape(MT, P, D).transpose(1, 0, 2).reshape(P, -1)
    rt = by_kt(np.concatenate([L0_ffn_router_weight, L0_ffn_shared_gate_w]).T)
    wc = np.concatenate([by_kt(gu), dn, rt], axis=1)
    wc = np.concatenate([wc, np.zeros((P, WC_CHUNKS * CH - wc.shape[1]), np.float32)], axis=1)
    arr["wC"] = wc.reshape(P, WC_CHUNKS, CH).transpose(1, 0, 2)
    arr.update(constants())
    return arr


def kernel(**inputs):
    import concourse.bacc as bacc
    from concourse.bass_utils import run_bass_kernel_spmd

    nc = bacc.Bacc("TRN2", target_bir_lowering=False, num_devices=1)
    arrays = {k: np.ascontiguousarray(v) for k, v in layout(**{k: np.asarray(v) for k, v in inputs.items()}).items()}
    aps = {k: nc.dram_tensor("in_" + k, v.shape, mybir.dt.from_np(v.dtype), kind="ExternalInput").ap() for k, v in arrays.items()}
    out = nc.dram_tensor("out", (T, D), F32, kind="ExternalOutput").ap()
    build(nc, aps, out)
    r = run_bass_kernel_spmd(nc, [{"in_" + k: v for k, v in arrays.items()}], core_ids=[0])
    return r.results[0]["out"].reshape(SEQS, L, D)
```

```python
from contextlib import ExitStack

import numpy as np

import concourse.bass as bass
from concourse import mybir

F32 = mybir.dt.float32
F16 = mybir.dt.float16
ALU = mybir.AluOpType
ACT = mybir.ActivationFunctionType
AX = mybir.AxisListType

P = 128
SEQS, L, D = 64, 64, 256
T = SEQS * L
TILES = T // P
KT = D // P
H, HKV, HD = 16, 4, 128
REP = H // HKV
GT = 4
GN = GT * P
GROUPS = TILES // GT
EPS = 1e-5

S_X, S_W, S_VO = 64.0, 256.0, 2048.0
S_V, S_P = 64.0, 1024.0
S_Y, S_C = 16.0, 16.0
S_H, S_CMB = 8.0, 256.0

XH, XD, XJ = 8, 8, 4
XS = XH // XJ
MAXROW = 3 * XD

E, I_MOE, I_SH = 8, 176, 704
MT = -(-(E * I_MOE + I_SH) // P)
HID = MT * P
WC_CHUNKS = 14
CH = 1024
GU_OFF, DN_OFF, RT_OFF = 0, KT * 2 * HID, KT * 2 * HID + MT * D


def wait_apart(eng, setup, *waits):
    for _, count in waits:
        if not isinstance(count, int):
            eng.compute_val(count)
    eng.wait_ge(*setup)
    for sem, count in waits:
        eng.wait_ge(sem, count)


def ln_statistics(nc, dve, tiles, mv, stats, step, done, group, setup):
    n = len(tiles)
    for j, src in enumerate(tiles):
        nc.vector.bn_stats(stats[:, j, :], src).then_inc(step, 1)
    for j in range(n):
        wait_apart(dve, setup, (step, n * group + j + 1))
        nc.vector.bn_aggr(mv[:, j, :], stats[:, j, :]).then_inc(done, 1)


def ln_rstd(nc, pool, mv, rstd, half, have, count, added, nth, done, setup, scale=1.0, waits=()):
    wait_apart(pool, setup, (have, count), *waits)
    nc.gpsimd.tensor_scalar(rstd[:, :], mv[:, :, 1], EPS, scale ** -2, ALU.add, ALU.mult).then_inc(added, 1)
    pool.wait_ge(added, nth)
    nc.gpsimd.tensor_tensor(rstd[:, :], rstd[:, :], half, ALU.pow).then_inc(done, 1)


def ln_normalise(nc, dve, src, dst, mv, rstd, j, done):
    nc.vector.tensor_scalar(dst, src, mv[:, j, 0:1], rstd[:, j:j + 1], ALU.subtract, ALU.mult).then_inc(done, 1)


def matmul3(nc, out, stat, mov, start, stop):
    nc.tensor.matmul(out, stat[0], mov[0], start=start, stop=False)
    nc.tensor.matmul(out, stat[0], mov[1], start=False, stop=False)
    return nc.tensor.matmul(out, stat[1], mov[0], start=False, stop=stop)


def block_a(nc, X, ident, a):
    with ExitStack() as ctx:
        def sb(name, shape, dt=F32):
            return ctx.enter_context(nc.sbuf_tensor(name, shape, dt))

        def sem(name):
            return ctx.enter_context(nc.semaphore(name))

        NCH = 10
        WH = sb("a_wh", [P, NCH, CH], F16)
        WL = sb("a_wl", [P, NCH, CH], F16)
        aT = sb("a_at", [P, 2, H, GN], F16)
        aTh, aTl = aT[:, 0], aT[:, 1]
        stage = aT[:, :, :, :].rearrange("p a h n -> p (a h n)").bitcast(F32).rearrange("p (s c) -> p s c", c=CH)
        NST = 8
        xhat = sb("a_xhat", [P, GT, D])
        stats = sb("a_stats", [P, GT, 6])
        mv = sb("a_mv", [P, GT, 2])
        rstd = sb("a_rstd", [P, GT])
        half = sb("a_half", [P, GT])
        xTh = sb("a_xth", [P, KT, GN], F16)
        xTl = sb("a_xtl", [P, KT, GN], F16)
        tabq = sb("a_tabq", [P, 2, L])
        tabk = sb("a_tabk", [P, 2, HD])
        kmul = sb("a_kmul", [P, 2, 2, HKV, HD])
        kext = sb("a_kext", [P, 2, HKV, HD + 1])
        kT = sb("a_kt", [P, GT, HKV, 2, P])
        V = sb("a_v", [P, 2, 2, GT, HKV * HD], F16)
        qCS = sb("a_qcs", [P, 2, 2, REP, GN])
        st = sb("a_st", [P, 2, 512])
        pr = sb("a_pr", [P, 2, 512])
        pT = sb("a_pt", [P, 2, 2, 512], F16)
        a32 = sb("a_a32", [P, 2, REP, P])
        sm = sb("a_sm", [P, 2, 3, 8])
        B = [ctx.enter_context(nc.psum_tensor(f"a_bank{n}", [P, 512], F32)) for n in range(8)]

        wa_in = [sem(f"a_wa_in{n}") for n in range(NST)]
        tab_in, w_hi, w_lo, v_zero = sem("a_tab_in"), sem("a_w_hi"), sem("a_w_lo"), sem("a_v_zero")
        x_in = [sem(f"a_x_in{n}") for n in range(GROUPS)]
        ln_add = sem("a_ln_add")
        ln_st, ln_mv, ln_rs, xhat_ok = sem("a_ln_st"), sem("a_ln_mv"), sem("a_ln_rs"), sem("a_xhat_ok")
        xtr, xT_hi, xT_lo = sem("a_xtr"), sem("a_xt_hi"), sem("a_xt_lo")
        k_proj, v_proj, q_proj = sem("a_k_proj"), sem("a_v_proj"), sem("a_q_proj")
        k_mul, k_ext, k_tr, k_T, v_ok = sem("a_k_mul"), sem("a_k_ext"), sem("a_k_tr"), sem("a_k_t"), sem("a_v_ok")
        k_wrap = sem("a_k_wrap")
        v_lo, p_T_lo, a_cp = sem("a_v_lo"), sem("a_p_t_lo"), sem("a_cp")
        q_rope = sem("a_q_rope")
        s_mm, s_copy, s_tr, s_max, s_sub, s_exp = (sem("a_" + n) for n in ("s_mm", "s_copy", "s_tr", "s_max", "s_sub", "s_exp"))
        s_sum, s_rec, p_ok, p_tr, p_T = (sem("a_" + n) for n in ("s_sum", "s_rec", "p_ok", "p_tr", "p_t"))
        pv, a_hi, a_lo, wo, x_new = (sem("a_" + n) for n in ("pv", "a_hi", "a_lo", "wo", "x_new"))

        block = ctx.enter_context(nc.Block())
        LAST = GROUPS - 1
        SETUP = (v_zero, 3)

        def in_loop(eng, body):
            body(0, False)
            with eng.Fori(1, LAST) as i:
                body(i, False)
            body(LAST, True)

        EARLY = 4

        def weight_scale(c):
            return S_VO if c == 1 or c >= 6 else S_W

        def next_xT_hi(act, base):
            for kt in range(KT):
                act.wait_ge(xtr, base + kt + 1)
                nc.scalar.activation(xTh[:, kt], B[6 + kt][:, :], ACT.Copy, scale=S_X).then_inc(xT_hi, 1)

        def head_cols(t, kv, p):
            return t[:, REP * kv:REP * kv + REP, p * P:(p + 1) * P]

        def pv_cols(bank):
            return bank[:, :].rearrange("p (b h q) -> p b h q", b=2, h=REP)

        @block.sync
        def _(sp):
            xg = a["x"].rearrange("(g t p) d -> g p t d", p=P, t=GT)
            sp.dma_start(X[:, 0:GT, :], xg[0]).then_inc(x_in[0], 16)
            sp.dma_start(tabq[:, :, :], a["tabq"].rearrange("p (a l) -> p a l", a=2)).then_inc(tab_in, 16)
            sp.dma_start(tabk[:, :, :], a["tabk"].rearrange("p (a l) -> p a l", a=2)).then_inc(tab_in, 16)
            sp.dma_start(ident[:, :], a["ident"]).then_inc(tab_in, 16)
            for c in range(NCH):
                if c >= NST:
                    sp.wait_ge(w_lo, c - NST + 1)
                sp.dma_start(stage[:, c % NST, :], a["wA"][c]).then_inc(wa_in[c % NST], 16)
            for g in range(1, GROUPS):
                sp.dma_start(X[:, g * GT:(g + 1) * GT, :], xg[g]).then_inc(x_in[g], 16)

        @block.gpsimd
        def _(pool):
            nc.gpsimd.memset(half[:, :], -0.5).then_inc(v_zero, 1)
            for s in range(2):
                pool.wait_ge(v_zero, s + 1)
                nc.gpsimd.memset(V[64 * (1 - s):64 * (1 - s) + 64, :, s, :, :], 0.0).then_inc(v_zero, 1)

            pool.wait_ge(v_zero, 3)
            ln_rstd(nc, pool, mv, rstd, half[:, :], ln_mv, GT, ln_add, 1, ln_rs, SETUP)

            def body(i, last):
                def rotate_k(j):
                    pool.wait_ge(k_mul, 4 * i + j + 1)
                    if j >= 2:
                        pool.wait_ge(k_tr, 8 * i + 2 * (j - 1))
                    else:
                        pool.wait_ge(k_tr, 8 * i)
                    b = j % 2
                    nc.gpsimd.tensor_tensor(kext[:, b, :, 0:HD], kmul[:, b, 0], kmul[:, b, 1], ALU.add).then_inc(k_wrap, 1)
                    wait_apart(pool, SETUP, (k_wrap, 4 * i + j + 1))
                    nc.gpsimd.tensor_copy(kext[:, b, :, HD:HD + 1], kext[:, b, :, 0:1]).then_inc(k_ext, 1)

                def normalise(kv):
                    for u in range(2):
                        n = 8 * i + 2 * kv + u
                        pool.wait_ge(s_rec, n + 1)
                        nc.gpsimd.tensor_tensor(pr[:, u].rearrange("p (g k) -> p g k", k=L), pr[:, u].rearrange("p (g k) -> p g k", k=L),
                                                sm[:, u, 2, :].unsqueeze(2).to_broadcast([P, 8, L]), ALU.mult).then_inc(p_ok, 1)

                def out_lo(kv, half):
                    for p in (2 * half, 2 * half + 1):
                        pool.wait_ge(a_hi, 16 * i + 4 * kv + p + 1)
                        nc.gpsimd.tensor_tensor(head_cols(aTl, kv, p), a32[:, p % 2], head_cols(aTh, kv, p), ALU.subtract).then_inc(a_lo, 1)

                for j in range(GT):
                    rotate_k(j)
                normalise(0)
                for kv in range(1, HKV - 1):
                    out_lo(kv - 1, 0)
                    normalise(kv)
                    out_lo(kv - 1, 1)
                out_lo(HKV - 2, 0)
                if not last:
                    used = (xhat_ok, GT * i + GT)
                    ln_rstd(nc, pool, mv, rstd, half[:, :], ln_mv, GT * i + 2 * GT, ln_add, i + 2, ln_rs, SETUP, waits=[used])
                normalise(HKV - 1)
                out_lo(HKV - 2, 1)
                out_lo(HKV - 1, 0)
                out_lo(HKV - 1, 1)

            in_loop(pool, body)

        @block.scalar
        def _(act):
            def weight_hi(c):
                act.wait_ge(wa_in[c % NST], 16 * (c // NST + 1))
                nc.scalar.activation(WH[:, c], stage[:, c % NST], ACT.Copy, scale=weight_scale(c)).then_inc(w_hi, 1)

            for c in range(EARLY):
                weight_hi(c)
                if c == 1:
                    next_xT_hi(act, 0)
            act.wait_ge(v_zero, 3)

            def body(i, last):
                def copy_v(j):
                    act.wait_ge(v_proj, 4 * i + j + 1)
                    act.wait_ge(pv, 16 * i)
                    for s in range(2):
                        rows = slice(64 * s, 64 * s + 64)
                        ins = nc.scalar.activation(V[rows, 0, s, j, :], B[6 + j % 2][rows, :], ACT.Copy, scale=S_V / (S_X * S_VO))
                    ins.then_inc(v_ok, 1)

                def copy_kT(j):
                    act.wait_ge(s_mm, 8 * i)
                    for b in range(2):
                        act.wait_ge(k_tr, 8 * i + 2 * j + b + 1)
                        nc.scalar.activation(kT[:, j, 2 * b:2 * b + 2].rearrange("p a c n -> p (a c n)"), B[4 + b][:, :], ACT.Copy).then_inc(k_T, 1)

                def copy_scores(kv):
                    for u in range(2):
                        n = 8 * i + 2 * kv + u
                        act.wait_ge(s_mm, n + 1)
                        if kv >= 1:
                            act.wait_ge(s_tr, n - 1)
                        else:
                            act.wait_ge(s_tr, 8 * i)
                        nc.scalar.activation(st[:, u], B[2 + u][:, :], ACT.Copy).then_inc(s_copy, 1)

                def exps(kv, *us):
                    for u in us:
                        act.wait_ge(s_sub, 8 * i + 2 * kv + u + 1)
                        nc.scalar.activation(pr[:, u], pr[:, u], ACT.Exp).then_inc(s_exp, 1)

                def copy_pT(kv):
                    for u in range(2):
                        n = 8 * i + 2 * kv + u
                        act.wait_ge(p_tr, n + 1)
                        if kv >= 1:
                            act.wait_ge(pv, 2 * (n - 1))
                        else:
                            act.wait_ge(pv, 16 * i)
                        nc.scalar.activation(pT[:, 0, u], B[4 + u][:, :], ACT.Copy, scale=S_P).then_inc(p_T, 1)

                def late_weights(*chunks):
                    if isinstance(i, int) and i == 0:
                        for c in chunks:
                            weight_hi(c)

                def out_hi(kv, *tiles):
                    if kv == 0 and 0 in tiles:
                        act.wait_ge(wo, 4 * i)
                        act.wait_ge(w_lo, NCH)
                    for p in tiles:
                        n = 16 * i + 4 * kv + p
                        act.wait_ge(pv, n + 1)
                        if 4 * kv + p >= 2:
                            act.wait_ge(a_lo, n - 1)
                        else:
                            act.wait_ge(a_lo, 16 * i)
                        nc.scalar.activation(a32[:, p % 2].rearrange("p h (b q) -> p b h q", b=2), pv_cols(B[6 + p % 2]),
                                             ACT.Copy, scale=1.0 / S_P).then_inc(a_cp, 1)
                        act.wait_ge(a_cp, n + 1)
                        nc.scalar.activation(head_cols(aTh, kv, p), a32[:, p % 2], ACT.Copy).then_inc(a_hi, 1)

                copy_v(0)
                copy_kT(0)
                late_weights(4)
                copy_v(1)
                late_weights(5)
                for j in range(1, GT):
                    copy_kT(j)
                    late_weights(*[(6,), (7,), (8, 9)][j - 1])
                for kv in range(HKV):
                    copy_scores(kv)
                    if kv == 0:
                        copy_v(2)
                        exps(0, 0, 1)
                        copy_v(3)
                    else:
                        out_hi(kv - 1, 0)
                        out_hi(kv - 1, 1)
                        exps(kv, 0)
                        exps(kv, 1)
                        out_hi(kv - 1, 2)
                        out_hi(kv - 1, 3)
                    copy_pT(kv)
                out_hi(HKV - 1, 0, 1, 2, 3)
                if not last:
                    next_xT_hi(act, 2 * i + 2)

            in_loop(act, body)

        @block.vector
        def _(dve):
            def tiles(group):
                return [X[:, bass.ds(GT * group + j, 1), :].rearrange("p o d -> p (o d)") for j in range(GT)]

            def normalise(group):
                dve.wait_ge(ln_rs, group + 1)
                for j, src in enumerate(tiles(group)):
                    ln_normalise(nc, dve, src, xhat[:, j, :], mv, rstd, j, xhat_ok)

            def xT_lo_parts(base):
                for kt in range(KT):
                    dve.wait_ge(xT_hi, base + kt + 1)
                    nc.vector.scalar_tensor_tensor(xTl[:, kt], B[6 + kt][:, :], S_X, xTh[:, kt], ALU.mult, ALU.subtract).then_inc(xT_lo, 1)

            dve.wait_ge(x_in[0], 16)
            ln_statistics(nc, dve, tiles(0), mv, stats, ln_st, ln_mv, 0, SETUP)
            normalise(0)

            def weight_lo(c):
                dve.wait_ge(w_hi, c + 1)
                nc.vector.scalar_tensor_tensor(WL[:, c], stage[:, c % NST], weight_scale(c), WH[:, c], ALU.mult, ALU.subtract).then_inc(w_lo, 1)

            for c in range(EARLY):
                weight_lo(c)
                if c == 1:
                    xT_lo_parts(0)
            dve.wait_ge(tab_in, 48)

            def body(i, last):
                def multiply_k(j):
                    b = j % 2
                    dve.wait_ge(k_proj, 4 * i + j + 1)
                    if j >= 2:
                        dve.wait_ge(k_wrap, 4 * i + j - 1)
                    else:
                        dve.wait_ge(k_wrap, 4 * i)
                    k = B[j % 2][:, :].rearrange("p (h d) -> p h d", h=HKV)
                    cos = tabk[:, 0, :].unsqueeze(1).to_broadcast([P, HKV, HD])
                    nc.vector.tensor_tensor(kmul[:, b, 0], k, cos, ALU.mult)
                    sin = tabk[:, 1, 1:HD].unsqueeze(1).to_broadcast([P, HKV, HD - 1])
                    nc.vector.tensor_tensor(kmul[:, b, 1, :, 1:HD], k[:, :, 0:HD - 1], sin, ALU.mult)
                    sin0 = tabk[:, 1, 0:1].unsqueeze(1).to_broadcast([P, HKV, 1])
                    nc.vector.tensor_tensor(kmul[:, b, 1, :, 0:1], k[:, :, HD - 1:HD], sin0, ALU.mult).then_inc(k_mul, 1)

                def rotate_q(h):
                    kv, r = h // REP, h % REP
                    dve.wait_ge(q_proj, 16 * i + h + 1)
                    if r == 0:
                        if kv >= 2:
                            dve.wait_ge(s_mm, 8 * i + 2 * (kv - 1))
                        else:
                            dve.wait_ge(s_mm, 8 * i)
                    q = B[h % 2][:, :].rearrange("p (b l) -> p b l", l=L)
                    for c in range(2):
                        table = tabq[:, c, :].unsqueeze(1).to_broadcast([P, GN // L, L])
                        ins = nc.vector.tensor_tensor(qCS[:, kv % 2, c, r].rearrange("p (b l) -> p b l", l=L), q, table, ALU.mult)
                    ins.then_inc(q_rope, 1)

                def subtract_max(kv):
                    for u in range(2):
                        n = 8 * i + 2 * kv + u
                        s = B[4 + u][:, :].rearrange("p (g k) -> p g k", k=L)
                        dve.wait_ge(s_tr, n + 1)
                        nc.vector.tensor_reduce(out=sm[:, u, 0, :].unsqueeze(2), in_=s, axis=AX.X, op=ALU.max).then_inc(s_max, 1)
                        dve.wait_ge(s_max, n + 1)
                        if kv >= 1:
                            dve.wait_ge(p_tr, n - 1)
                        else:
                            dve.wait_ge(p_tr, 8 * i)
                        nc.vector.tensor_tensor(pr[:, u].rearrange("p (g k) -> p g k", k=L), s,
                                                sm[:, u, 0, :].unsqueeze(2).to_broadcast([P, 8, L]), ALU.subtract).then_inc(s_sub, 1)

                def row_sums(kv):
                    for u in range(2):
                        n = 8 * i + 2 * kv + u
                        dve.wait_ge(s_exp, n + 1)
                        nc.vector.tensor_reduce(out=sm[:, u, 1, :].unsqueeze(2), in_=pr[:, u].rearrange("p (g k) -> p g k", k=L),
                                                axis=AX.X, op=ALU.add).then_inc(s_sum, 1)
                        dve.wait_ge(s_sum, n + 1)
                        nc.vector.reciprocal(sm[:, u, 2, :], sm[:, u, 1, :]).then_inc(s_rec, 1)

                def v_lo_part(j):
                    dve.wait_ge(v_ok, 4 * i + j + 1)
                    for s in range(2):
                        rows = slice(64 * s, 64 * s + 64)
                        ins = nc.vector.scalar_tensor_tensor(V[rows, 1, s, j, :], B[6 + j % 2][rows, :], S_V / (S_X * S_VO),
                                                             V[rows, 0, s, j, :], ALU.mult, ALU.subtract)
                    ins.then_inc(v_lo, 1)

                def pT_lo(kv):
                    for u in range(2):
                        dve.wait_ge(p_T, 8 * i + 2 * kv + u + 1)
                        nc.vector.scalar_tensor_tensor(pT[:, 1, u], B[4 + u][:, :], S_P, pT[:, 0, u], ALU.mult, ALU.subtract).then_inc(p_T_lo, 1)

                def late_weights(*chunks):
                    if isinstance(i, int) and i == 0:
                        for c in chunks:
                            weight_lo(c)

                multiply_k(0)
                multiply_k(1)
                late_weights(4)
                multiply_k(2)
                late_weights(5)
                multiply_k(3)
                for h in range(REP):
                    rotate_q(h)
                v_lo_part(0)
                late_weights(6, 7, 8, 9)
                for kv in range(HKV - 1):
                    rotate_q(REP * (kv + 1))
                    if kv:
                        pT_lo(kv - 1)
                    rotate_q(REP * (kv + 1) + 1)
                    if kv == 0:
                        v_lo_part(1)
                    rotate_q(REP * (kv + 1) + 2)
                    subtract_max(kv)
                    row_sums(kv)
                    rotate_q(REP * (kv + 1) + 3)
                    if kv == 0:
                        v_lo_part(2)
                        v_lo_part(3)
                pT_lo(HKV - 2)
                subtract_max(HKV - 1)
                if isinstance(i, int) and i == 0:
                    for g in range(1, GROUPS):
                        dve.wait_ge(x_in[g], 16)
                if not last:
                    ln_statistics(nc, dve, tiles(i + 1), mv, stats, ln_st, ln_mv, i + 1, SETUP)
                row_sums(HKV - 1)
                if not last:
                    dve.wait_ge(xtr, 2 * i + 2)
                    normalise(i + 1)
                pT_lo(HKV - 1)
                if not last:
                    xT_lo_parts(2 * i + 2)
                for j in range(GT):
                    dve.wait_ge(wo, 4 * i + j + 1)
                    xj = X[:, bass.ds(GT * i + j, 1), :].rearrange("p o d -> p (o d)")
                    nc.vector.scalar_tensor_tensor(xj, B[j][:, 0:D], 1.0 / (S_V * S_VO), xj, ALU.mult, ALU.add).then_inc(x_new, 1)

            in_loop(dve, body)

        @block.tensor
        def _(pe):
            def transpose_xhat(base):
                for j in range(GT):
                    pe.wait_ge(xhat_ok, 4 * base + j + 1)
                    for kt in range(KT):
                        ins = nc.tensor.transpose(B[6 + kt][:, j * P:(j + 1) * P], xhat[:, j, kt * P:(kt + 1) * P], ident[:, :])
                        if j == GT - 1:
                            ins.then_inc(xtr, 1)

            def w(c, lo, n, kt=0):
                cols = slice(kt * 512 + lo, kt * 512 + lo + n)
                return (WH[:, c, cols], WL[:, c, cols])

            pe.wait_ge(tab_in, 48)
            transpose_xhat(0)

            def body(i, last):
                def project_tokens(j, c, bank, done):
                    for kt in range(KT):
                        x = (xTh[:, kt, j * P:(j + 1) * P], xTl[:, kt, j * P:(j + 1) * P])
                        ins = matmul3(nc, bank[:, :], x, w(c, 0, 512, kt), kt == 0, kt == KT - 1)
                    ins.then_inc(done, 1)

                def project_k(j):
                    if j >= 2:
                        pe.wait_ge(k_mul, 4 * i + j - 1)
                    project_tokens(j, 0, B[j % 2], k_proj)

                def project_v(j):
                    if j >= 2:
                        pe.wait_ge(v_lo, 4 * i + j - 1)
                    project_tokens(j, 1, B[6 + j % 2], v_proj)

                def transpose_k(j):
                    pe.wait_ge(k_ext, 4 * i + j + 1)
                    if j >= 1:
                        pe.wait_ge(k_T, 8 * i + 2 * j)
                    else:
                        pe.wait_ge(p_T_lo, 8 * i)
                    for b in range(2):
                        for kv in range(2):
                            for c in range(2):
                                o = (2 * kv + c) * P
                                ins = nc.tensor.transpose(B[4 + b][:, o:o + P], kext[:, j % 2, 2 * b + kv, c:c + HD], ident[:, :])
                        ins.then_inc(k_tr, 1)

                def project_q(h):
                    if isinstance(i, int) and i == 0 and h % REP == 0:
                        pe.wait_ge(w_lo, 3 + h // REP)
                    if h < 2:
                        pe.wait_ge(k_mul, 4 * i + 3 + h)
                    else:
                        pe.wait_ge(q_rope, 16 * i + h - 1)
                    for kt in range(KT):
                        ins = matmul3(nc, B[h % 2][:, :], w(2 + h // REP, (h % REP) * HD, HD, kt), (xTh[:, kt], xTl[:, kt]), kt == 0, kt == KT - 1)
                    ins.then_inc(q_proj, 1)

                def scores(kv):
                    pe.wait_ge(q_rope, 16 * i + REP * kv + REP)
                    if kv == 0:
                        pe.wait_ge(x_new, 4 * i)
                    for u in range(2):
                        if kv == 0:
                            pe.wait_ge(k_T, 8 * i + 4 * u + 4)
                        else:
                            pe.wait_ge(s_copy, 8 * i + 2 * kv + u - 1)
                        for pp in range(2):
                            p = 2 * u + pp
                            for c in range(2):
                                for s in range(2):
                                    rows = slice(64 * s, 64 * s + 64)
                                    ins = nc.tensor.matmul(B[2 + u][rows, pp * 256:(pp + 1) * 256], kT[:, p, kv, c, rows],
                                                           qCS[:, kv % 2, c, :, p * P + 64 * s:p * P + 64 * s + 64], start=c == 0, stop=c == 1)
                        ins.then_inc(s_mm, 1)

                def transpose_scores(kv):
                    for u in range(2):
                        n = 8 * i + 2 * kv + u
                        pe.wait_ge(s_copy, n + 1)
                        if kv == 0:
                            pe.wait_ge(k_T, 8 * i + 8)
                        else:
                            pe.wait_ge(p_T_lo, n - 1)
                        for b in range(4):
                            ins = nc.tensor.transpose(B[4 + u][:, b * P:(b + 1) * P], st[:, u, b * P:(b + 1) * P], ident[:, :])
                        ins.then_inc(s_tr, 1)

                def transpose_probs(kv):
                    for u in range(2):
                        pe.wait_ge(p_ok, 8 * i + 2 * kv + u + 1)
                        for b in range(4):
                            ins = nc.tensor.transpose(B[4 + u][:, b * P:(b + 1) * P], pr[:, u, b * P:(b + 1) * P], ident[:, :])
                        ins.then_inc(p_tr, 1)

                def values(kv, half):
                    if kv == 0 and half == 0:
                        pe.wait_ge(v_lo, 4 * i + 4)
                    for p in (2 * half, 2 * half + 1):
                        n = 16 * i + 4 * kv + p
                        pe.wait_ge(p_T_lo, 8 * i + 2 * kv + p // 2 + 1)
                        if 4 * kv + p >= 2:
                            pe.wait_ge(a_cp, n - 1)
                        else:
                            pe.wait_ge(a_cp, 16 * i)
                        for s in range(2):
                            v = tuple(V[:, part, s, p, kv * HD:(kv + 1) * HD] for part in range(2))
                            probs = tuple(pT[:, part, p // 2, (p % 2) * 256:(p % 2 + 1) * 256] for part in range(2))
                            ins = matmul3(nc, B[6 + p % 2][:, s * 256:(s + 1) * 256], v, probs, True, True)
                        ins.then_inc(pv, 1)

                def project_out(j, h0, h1):
                    if isinstance(i, int) and i == 0 and h0 == 0:
                        pe.wait_ge(w_lo, NCH)
                    if h0 == 0:
                        if j < 2:
                            pe.wait_ge(q_rope, 16 * i + 15 + j)
                        else:
                            pe.wait_ge(s_copy, 8 * i + 5 + j)
                    for h in range(h0, h1):
                        if h % REP == 0:
                            pe.wait_ge(a_lo, 16 * i + h + j + 1)
                        stat = (aTh[:, h, j * P:(j + 1) * P], aTl[:, h, j * P:(j + 1) * P])
                        ins = matmul3(nc, B[j][:, 0:D], stat, wo_cols(h), h == 0, h == H - 1)
                    if h1 == H:
                        ins.then_inc(wo, 1)

                def wo_cols(h):
                    c, o = 6 + h // 4, (h % 4) * D
                    return (WH[:, c, o:o + D], WL[:, c, o:o + D])

                pe.wait_ge(xT_lo, 2 * i + 2)
                if not isinstance(i, int) or i > 0:
                    pe.wait_ge(x_new, 4 * i - 2)
                pe.wait_ge(w_lo, 2)
                project_k(0)
                project_k(1)
                project_v(0)
                project_k(2)
                transpose_k(0)
                project_v(1)
                project_k(3)
                transpose_k(1)
                project_q(0)
                project_q(1)
                transpose_k(2)
                project_q(2)
                project_q(3)
                transpose_k(3)
                project_q(4)
                project_q(5)
                done = H - REP
                for kv in range(HKV):
                    scores(kv)
                    if kv < HKV - 1:
                        project_q(REP * (kv + 1) + 2)
                    transpose_scores(kv)
                    if kv == 0:
                        project_v(2)
                        project_v(3)
                    else:
                        values(kv - 1, 0)
                    if kv < HKV - 1:
                        project_q(REP * (kv + 1) + 3)
                    else:
                        project_out(1, 0, done - REP)
                    if kv > 0:
                        values(kv - 1, 1)
                    if kv < HKV - 2:
                        project_q(REP * (kv + 2))
                    if kv == HKV - 2:
                        project_out(0, 0, done - REP)
                    if kv == HKV - 1:
                        project_out(0, done - REP, done)
                    transpose_probs(kv)
                    if kv < HKV - 2:
                        project_q(REP * (kv + 2) + 1)
                project_out(1, done - REP, done)
                values(HKV - 1, 0)
                project_out(2, 0, done - REP)
                values(HKV - 1, 1)
                project_out(2, done - REP, done)
                if not last:
                    pe.wait_ge(a_cp, 16 * i + 16)
                    transpose_xhat(i + 1)
                project_out(0, done, H)
                project_out(1, done, H)
                project_out(2, done, H)
                project_out(3, 0, H)

            in_loop(pe, body)


def block_b(nc, X, ident, WCh, WCl, a):
    with ExitStack() as ctx:
        def sb(name, shape, dt=F32):
            return ctx.enter_context(nc.sbuf_tensor("b_" + name, shape, dt))

        def sem(name):
            return ctx.enter_context(nc.semaphore("b_" + name))

        RING = 4
        Q = D
        y = sb("y", [P, 2, D])
        y32 = sb("y32", [P, 4, Q])
        c32 = sb("c32", [P, 4, Q])
        hm = sb("hm", [P, 2, 2 * Q], F16)
        yst = sb("yst", [P, RING, XS, Q], F16)
        kst = sb("kst", [P, 2, XS * Q], F16)
        kz = sb("kz", [P, RING, XJ, XS * Q], F16)
        vin = sb("vin", [P, 2, 2, 64])
        vst = sb("vst", [P, 2, 2, 2, XH, 32])
        pr = sb("pr", [P, 8, 512])
        mx = sb("mx", [P, 4, 8])
        mrow = sb("mrow", [XJ, 4, Q], F16)
        num = sb("num", [P, 2, 512])
        rec = sb("rec", [P, 2, 2, XJ])
        ret = sb("ret", [P, 2, 2, 64])
        gamma = sb("gamma", [P, 1])
        mask = sb("mask", [P, 2])
        stats = sb("stats", [P, 1, 6])
        mv = sb("mv", [P, 1, 2])
        rstd = sb("rstd", [P, 1])
        half = sb("half", [P, 1])
        wst = sb("wst", [P, CH])
        B = [ctx.enter_context(nc.psum_tensor(f"b_bank{n}", [P, 512], F32)) for n in range(8)]

        cst_in, zeroed, kz_zero, pool_init = sem("cst_in"), sem("zeroed"), sem("kz_zero"), sem("pool_init")
        ln_st, ln_mv, ln_add, ln_rs, y_ok = (sem(n) for n in ("ln_st", "ln_mv", "ln_add", "ln_rs", "y_ok"))
        y_out, y_in, c_in, v_in = sem("y_out"), sem("y_in"), sem("c_in"), sem("v_in")
        hm_y, y_cv, hm_k, k_cv, v_cv = sem("hm_y"), sem("y_cv"), sem("hm_k"), sem("k_cv"), sem("v_cv")
        kz_in = [sem(f"kz_in{n}") for n in range(RING)]
        m_mm, m_red, m_tr, m_row = sem("m_mm"), sem("m_red"), sem("m_tr"), sem("m_row")
        m_in = [sem(f"m_in{n}") for n in range(4)]
        e_mm, e_exp, pv, pv_ok = sem("e_mm"), sem("e_exp"), sem("pv"), sem("pv_ok")
        n_tr, n_rec, r_ok, r_tr, x_new = sem("n_tr"), sem("n_rec"), sem("r_ok"), sem("r_tr"), sem("x_new")
        c_sc, w_in, w_sc, w_hi, w_lo = sem("c_sc"), sem("w_in"), sem("w_sc"), sem("w_hi"), sem("w_lo")

        block = ctx.enter_context(nc.Block())
        SETUP = (cst_in, 32)
        PAIRS = TILES
        UN = 8
        ROUNDS = SEQS * XS // UN
        AHEAD = 3
        DMAS_Y, DMAS_K = XJ, XJ

        def in_loop(eng, body):
            body(0, True, 2)
            with eng.Fori(1, ROUNDS - 2) as i:
                body(i, False, 2)
            body(ROUNDS - 2, False, 1)
            body(ROUNDS - 1, False, 0)

        TURN = ((0, 1, 2, 0), (1, 2, 0, 1))
        AGO = ((2, 2, 5, 3), (3, 3, 3, 3))

        def max_comes(t, first, last):
            return not (first and t == 0) and not (last and t - 1 + AHEAD >= UN)

        def xtile(p):
            return X[:, bass.ds(p, 1), :].rearrange("p o d -> p (o d)")

        y_dram = nc.dram_tensor("y_rows", (2, XJ * XD, 2 * XS, D), F32, kind="Internal").ap()

        @block.sync
        def _(sp):
            def load_ctx(p):
                sp.wait_ge(k_cv, 2 * p)
                sp.dma_start(c32[:, :, :], a["ctxS"][bass.ds(p, 1)].rearrange("o p s q -> (o p) s q")).then_inc(c_in, 16)

            def load_values(p):
                sp.wait_ge(v_cv, p)
                sp.dma_start(vin[:, :, :, :], a["ctxT"][bass.ds(p, 1)].rearrange("o p (t b c) -> (o p) t b c", t=2, b=2)).then_inc(v_in, 16)

            def store_y(p, par):
                in_dram = [] if isinstance(p, int) and p < 2 else [(y_in, 16 * DMAS_Y * (p - 1))]
                wait_apart(sp, SETUP, (y_ok, p + 1), *in_dram)
                sp.dma_start(y_dram[par].rearrange("r s q -> s r q"), y[:, par, :]).then_inc(y_out, 16)

            def stack_y(p, par):
                sp.wait_ge(y_out, 16 * (p + 1))
                sp.wait_ge(y_cv, 2 * p)
                rows = y_dram[par].rearrange("(j d) s q -> j d (s q)", j=XJ)
                for j in range(XJ):
                    three = rows[j].unsqueeze(0).to_broadcast([3, XD, 4 * Q])
                    sp.dma_start(y32[32 * j:32 * j + 3 * XD, :, :].rearrange("p s q -> p (s q)"), three).then_inc(y_in, 16)

            def spread_k(b, r, *waits):
                wait_apart(sp, SETUP, (k_cv, b + 1), *waits)
                for j in range(XJ):
                    rows = slice(32 * j, 32 * j + 32)
                    sp.dma_start(kz[rows, r, j, :], kst[rows, r % 2, :]).then_inc(kz_in[r], 16)

            sp.dma_start(gamma[:, :], a["gamma"].to_broadcast([P, 1])).then_inc(cst_in, 16)
            sp.dma_start(mask[:, :], a["maskB"]).then_inc(cst_in, 16)
            load_ctx(0)
            store_y(0, 0)
            for p in range(2):
                if p == 0:
                    sp.wait_ge(zeroed, 1)
                else:
                    load_ctx(1)
                stack_y(p, p)
                if p == 0:
                    store_y(1, 1)
                    sp.wait_ge(kz_zero, 1)
                for q in range(2):
                    spread_k(2 * p + q, 2 * p + q)
                load_values(p)
            load_ctx(2)
            store_y(2, 0)

            def body(i, first, left):
                last = left == 0
                for t in range(UN):
                    s, p, q = UN * i + t, 2 * i + t // 4, t // 4
                    if t % 4 == 0 and not last:
                        stack_y(p + 2, q)
                    if t % 4 == 0 and not (first and t == 0) and not (last and t == 4):
                        load_values(p + 1)
                    if t == 0 and not first and not last:
                        sp.wait_ge(w_lo, i)
                        sp.dma_start(wst[:, :], a["wC"][bass.ds(i - 1, 1)].rearrange("o p n -> (o p) n")).then_inc(w_in, 16)
                    if t % 4 == 3 and left > q:
                        load_ctx(p + 3)
                        store_y(p + 3, 1 - q)
                    if t % 2 == 1 and not last:
                        spread_k(4 * i + (t - 1) // 2 + RING, (t - 1) // 2, (e_mm, 4 * s + 4))

            in_loop(sp, body)

        @block.gpsimd
        def _(pool):
            def convert_y(b, q, r, *waits):
                src = y32[:, 2 * q:2 * q + 2, :].rearrange("p s q -> p (s q)")
                wait_apart(pool, SETUP, (y_in, 8 * DMAS_Y * (b - q + 2)), (y_cv, b), *waits)
                nc.gpsimd.tensor_scalar(hm[:, 0], src, mask[:, 0:1], 1.0, ALU.mult, ALU.mult).then_inc(hm_y, 1)
                pool.wait_ge(hm_y, b + 1)
                nc.gpsimd.tensor_tensor(yst[:, r].rearrange("p s q -> p (s q)"), src, hm[:, 0], ALU.subtract).then_inc(y_cv, 1)

            def convert_k(b, q, *waits):
                src = c32[:, 2 * q:2 * q + 2, :].rearrange("p s q -> p (s q)")
                wait_apart(pool, SETUP, (c_in, 8 * (b - q + 2)))
                nc.gpsimd.tensor_scalar(src, src, S_C, 1.0, ALU.mult, ALU.mult).then_inc(c_sc, 1)
                wait_apart(pool, SETUP, (c_sc, b + 1), (k_cv, b))
                nc.gpsimd.tensor_scalar(hm[:, 1], src, mask[:, 1:2], 1.0, ALU.mult, ALU.mult).then_inc(hm_k, 1)
                pool.wait_ge(hm_k, b + 1)
                for sem, count in waits:
                    pool.wait_ge(sem, count)
                nc.gpsimd.tensor_tensor(kst[:, q, :], src, hm[:, 1], ALU.subtract).then_inc(k_cv, 1)

            def convert_v(p, par, *waits):
                wait_apart(pool, SETUP, (v_in, 16 * (p + 1)), *waits)
                nc.gpsimd.tensor_scalar(vst[:, par].rearrange("p t b h e -> p (t b h) e")[:, :, 0:XD],
                                        vin[:, :, :, :].rearrange("p t b (h d) -> p (t b h) d", d=XD),
                                        1.0, 0.0, ALU.mult, ALU.add).then_inc(v_cv, 1)

            def rstd_of(p):
                ln_rstd(nc, pool, mv, rstd, half[:, :], ln_mv, p + 1, ln_add, p + 1, ln_rs, SETUP, S_Y, [(y_ok, p)])

            nc.gpsimd.memset(half[:, :], -0.5).then_inc(pool_init, 1)
            nc.gpsimd.memset(wst[:, 0:1], 0.0).then_inc(w_lo, 1)
            pool.wait_ge(pool_init, 1)
            pool.wait_ge(cst_in, 32)
            rstd_of(0)
            rstd_of(1)
            nc.gpsimd.memset(y32[:, :, :], 0.0).then_inc(zeroed, 1)
            for b in range(RING):
                convert_k(b, b % 2, *([(kz_in[b - 2], 16 * DMAS_K)] if b >= 2 else []))
                if b == 0:
                    rstd_of(2)
                    nc.gpsimd.memset(vst[:, :, :, :, :, :], 0.0).then_inc(pool_init, 1)
                convert_y(b, b % 2, b)
                if b == 1:
                    pool.wait_ge(pool_init, 2)
                    nc.gpsimd.memset(vst[:, :, :, :, :, XD:XD + 1].rearrange("p a t b h e -> p (a t b h) e"), 1.0).then_inc(pool_init, 1)
                    pool.wait_ge(pool_init, 3)
                    convert_v(0, 0)

            def body(i, first, left):
                last = left == 0
                for q in range(2):
                    p, s0 = 2 * i + q, UN * i + 4 * q

                    def kst_spread(e):
                        r = 2 * q + 2 + e
                        return kz_in[r % RING], 16 * DMAS_K * (i + r // RING + 1)

                    chunk = bass.ds(i - 1, 1)
                    if not last:
                        convert_k(2 * p + 4, 0, kst_spread(0))
                    if left > q:
                        rstd_of(p + 3)
                    if not last:
                        convert_y(2 * p + 4, 0, 2 * q, (e_mm, 4 * (s0 + 2)))
                        convert_k(2 * p + 5, 1, kst_spread(1))
                    if not (last and q == 1):
                        convert_v(p + 1, (q + 1) % 2, *([] if first and q == 0 else [(pv, s0)]))
                    if q == 0 and not first and not last:
                        wait_apart(pool, SETUP, (w_in, 16 * i))
                        nc.gpsimd.tensor_scalar(wst[:, :], wst[:, :], S_W, 1.0, ALU.mult, ALU.mult).then_inc(w_sc, 1)
                    if q == 1 and not first and not last:
                        pool.wait_ge(w_hi, i)
                        hi = WCh[:, chunk, :].rearrange("p o n -> p (o n)")
                        nc.gpsimd.tensor_tensor(WCl[:, chunk, :].rearrange("p o n -> p (o n)"), wst[:, :], hi, ALU.subtract).then_inc(w_lo, 1)
                    if not last:
                        convert_y(2 * p + 5, 1, 2 * q + 1, (e_mm, 4 * (s0 + 4)))

            in_loop(pool, body)

        @block.scalar
        def _(act):
            def copy_max(s, t):
                act.wait_ge(m_tr, s + 1)
                if not (isinstance(s, int) and s < 4):
                    act.wait_ge(m_in[t % 4], 4 * (s - t % 4))
                nc.scalar.activation(mrow[:, t % 4, :], B[2][0:XJ, 0:Q], ACT.Copy, scale=-1.0 / (S_Y * S_C)).then_inc(m_row, 1)

            def insert_max(s, t):
                act.wait_ge(m_row, s + 1)
                act.dma_start(yst[MAXROW:P:32, t // 2 % RING, t % 2, :], mrow[:, t % 4, :]).then_inc(m_in[t % 4], 16)

            def copy_numerators(b, par):
                act.wait_ge(pv, 2 * b + 2)
                if not (isinstance(b, int) and b < 2):
                    act.wait_ge(n_tr, b - 1)
                nc.scalar.activation(num[:, par, :], B[6][:, :], ACT.Copy).then_inc(pv_ok, 1)

            for s in range(AHEAD):
                copy_max(s, s)
                insert_max(s, s)

            def body(i, first, left):
                last = left == 0
                for t in range(UN):
                    s = UN * i + t
                    for k in range(XJ):
                        act.wait_ge(e_mm, 4 * s + k + 1)
                        if k == 0 and not (first and t < 2):
                            act.wait_ge(pv, s - 1)
                        nc.scalar.activation(pr[:, 4 * (t % 2) + k, :], B[3 + TURN[t % 2][k]][:, :], ACT.Exp,
                                             scale=1.0 / (S_Y * S_C * float(np.sqrt(XD)))).then_inc(e_exp, 1)
                        if k == 1 and max_comes(t, first, last):
                            copy_max(s - 1 + AHEAD, (t - 1 + AHEAD) % UN)
                        if k == 2 and max_comes(t, first, last):
                            insert_max(s - 1 + AHEAD, (t - 1 + AHEAD) % UN)
                    if t % 2 == 0 and not (first and t == 0):
                        copy_numerators(4 * i + t // 2 - 1, (t // 2 - 1) % 2)
                    if t == 5 and not first and not last:
                        act.wait_ge(w_sc, i)
                        nc.scalar.activation(WCh[:, bass.ds(i - 1, 1), :].rearrange("p o n -> p (o n)"), wst[:, :], ACT.Copy).then_inc(w_hi, 1)

            in_loop(act, body)
            copy_numerators(SEQS - 1, 1)

        @block.vector
        def _(dve):
            def statistics(p):
                ln_statistics(nc, dve, [xtile(p)], mv, stats, ln_st, ln_mv, p, SETUP)

            def normalise(p, par):
                dve.wait_ge(ln_rs, p + 1)
                if not (isinstance(p, int) and p < 2):
                    dve.wait_ge(y_out, 16 * (p - 1))
                ln_normalise(nc, dve, xtile(p), y[:, par, :], mv, rstd, 0, y_ok)

            def reduce_max(s, t, k):
                dve.wait_ge(m_mm, 4 * s + k + 1)
                if k == 0 and not (isinstance(s, int) and s < 4):
                    dve.wait_ge(m_tr, s - 3)
                nc.vector.tensor_reduce(out=mx[:, t % 4, k::XJ].unsqueeze(2), in_=B[k % 2][:, :].rearrange("p (t l) -> p t l", t=2),
                                        axis=AX.X, op=ALU.max).then_inc(m_red, 1)

            def divide(b, q, pair):
                dve.wait_ge(n_tr, b + 1)
                v = B[7][:, :].rearrange("p (h t j r) -> p h t j r", h=2, t=2, j=XJ)
                nc.vector.reciprocal(rec[:, :, :, :].unsqueeze(4), v[:, :, :, :, XD:XD + 1]).then_inc(n_rec, 1)
                dve.wait_ge(n_rec, b + 1)
                if q == 0:
                    dve.wait_ge(r_tr, pair)
                for t in range(2):
                    ins = nc.vector.tensor_tensor(ret[:, t, q, :].rearrange("p (h j d) -> p h j d", h=2, j=XJ), v[:, :, t, :, 0:XD],
                                                  rec[:, :, t, :].unsqueeze(3).to_broadcast([P, 2, XJ, XD]), ALU.mult)
                ins.then_inc(r_ok, 1)

            def add_output(p):
                dve.wait_ge(r_tr, p + 1)
                nc.vector.scalar_tensor_tensor(xtile(p), B[7][:, 0:D], gamma[:, 0:1], xtile(p), ALU.mult, ALU.add).then_inc(x_new, 1)

            for p in range(3):
                statistics(p)
                if p == 2:
                    nc.vector.memset(kz[:, :, :, :], 0.0).then_inc(kz_zero, 1)
                normalise(p, p % 2)
            for s in range(AHEAD):
                for k in range(XJ):
                    reduce_max(s, s, k)
            dve.wait_ge(cst_in, 32)

            def body(i, first, left):
                last = left == 0
                for t in range(UN):
                    s = UN * i + t
                    more = not (last and t + AHEAD >= UN)
                    for k in range(XJ):
                        if more:
                            reduce_max(s + AHEAD, (t + AHEAD) % UN, k)
                        if k == 2 and t % 4 == 0 and left > t // 4:
                            statistics(2 * i + t // 4 + 3)
                        if k == 3 and t % 2 == 1 and not (first and t < 3):
                            b = 4 * i + (t - 3) // 2
                            divide(b, ((t - 3) // 2) % 2, 2 * i + (t - 3) // 4)
                        if k == 3 and t % 4 == 2 and not (first and t < 6):
                            add_output(2 * i + (t - 6) // 4)
                    if t % 4 == 3 and left > t // 4:
                        normalise(2 * i + t // 4 + 3, 1 - t // 4)

            in_loop(dve, body)
            divide(SEQS - 1, 1, PAIRS - 1)
            add_output(PAIRS - 1)

        @block.tensor
        def _(pe):
            def maxima_scores(i, t, k):
                r, h, g = t // 2 % RING, t % 2, 4 * (UN * i + t) + k
                if k == 0 and t % 2 == 0:
                    pe.wait_ge(y_cv, 4 * i + t // 2 + 1)
                    pe.wait_ge(kz_in[r], 16 * DMAS_K * (i + t // UN + 1))
                if not (isinstance(g, int) and g < 2):
                    pe.wait_ge(m_red, g - 1)
                for q in range(2):
                    ins = nc.tensor.matmul(B[k % 2][:, q * Q:(q + 1) * Q], yst[:, r, h, q * P:(q + 1) * P],
                                           kz[:, r, k, h * Q:(h + 1) * Q], start=True, stop=True)
                ins.then_inc(m_mm, 1)

            def scores(s, t, k):
                r, h, g = t // 2, t % 2, 4 * s + k
                if k == 0:
                    pe.wait_ge(m_in[t % 4], 4 * (s - t % 4) + 16)
                ago = AGO[t % 2][k]
                if not (isinstance(g, int) and g < ago):
                    pe.wait_ge(e_exp, g - ago + 1)
                for l in range(2):
                    ins = nc.tensor.matmul(B[3 + TURN[t % 2][k]][:, l * Q:(l + 1) * Q], kz[:, r, k, h * Q + l * P:h * Q + (l + 1) * P],
                                           yst[:, r, h, :], start=True, stop=True)
                ins.then_inc(e_mm, 1)

            def products(i, t, l):
                v, h, par = t // 2 % 2, t % 2, t // 4 % 2
                if l == 0:
                    pe.wait_ge(e_exp, 4 * (UN * i + t) + 4)
                if l == 0 and t % 4 == 0:
                    pe.wait_ge(v_cv, 2 * i + t // 4 + 1)
                if l == 0 and h == 0:
                    pe.wait_ge(pv_ok, 4 * i + t // 2)
                for j in range(XJ):
                    ins = nc.tensor.matmul(B[6][32 * j:32 * j + 32, h * Q:(h + 1) * Q], vst[:, par, l, v, XJ * h + j, :],
                                           pr[:, 4 * (t % 2) + j, l * Q:(l + 1) * Q], start=l == 0, stop=l == 1)
                if l == 1:
                    ins.then_inc(pv, 1)

            def transpose_max(s, t):
                pe.wait_ge(m_red, 4 * s + 4)
                for q in range(2):
                    ins = nc.tensor.transpose(B[2][0:XJ, q * P:(q + 1) * P], mx[:, t % 4, XJ * q:XJ * q + XJ], ident[:, :])
                ins.then_inc(m_tr, 1)

            def transpose_numerators(b, par):
                pe.wait_ge(pv_ok, b + 1)
                for h in range(2):
                    for t in range(2):
                        o = (2 * h + t) * P
                        ins = nc.tensor.transpose(B[7][:, o:o + P], num[:, par, h * Q + t * P:h * Q + (t + 1) * P], ident[:, :])
                ins.then_inc(n_tr, 1)

            def transpose_output(p):
                pe.wait_ge(r_ok, 2 * p + 2)
                for t in range(2):
                    ins = nc.tensor.transpose(B[7][:, t * P:(t + 1) * P], ret[:, t].rearrange("p b c -> p (b c)"), ident[:, :])
                ins.then_inc(r_tr, 1)

            for s in range(AHEAD):
                for k in range(XJ):
                    maxima_scores(0, s, k)
                if s >= 1:
                    pe.wait_ge(m_row, s)
                transpose_max(s, s)

            def body(i, first, left):
                last = left == 0
                for t in range(UN):
                    s = UN * i + t
                    more = not (last and t + AHEAD >= UN)
                    divides = t % 2 == 1 and not (first and t < 3)
                    outputs = t % 4 == 2 and not (first and t < 6)
                    for k in range(XJ):
                        if more:
                            maxima_scores(i, t + AHEAD, k)
                        scores(s, t, k)
                        if k == 1 and max_comes(t, first, last):
                            pe.wait_ge(m_row, s - 1 + AHEAD)
                            transpose_max(s - 1 + AHEAD, (t - 1 + AHEAD) % UN)
                        if k % 2 == 1 and not (first and t == 0):
                            products(i if t else i - 1, (t - 1) % UN, k // 2)
                        if k == 2 and (divides or outputs):
                            if divides:
                                if t % 4 == 1:
                                    pe.wait_ge(r_ok, 4 * i + (t - 3) // 2)
                                elif not first or t > 3:
                                    pe.wait_ge(x_new, 2 * i + (t - 7) // 4 + 1)
                                transpose_numerators(4 * i + (t - 3) // 2, ((t - 3) // 2) % 2)
                            else:
                                transpose_output(2 * i + (t - 6) // 4)

            in_loop(pe, body)
            for l in range(2):
                products(ROUNDS - 1, UN - 1, l)
            pe.wait_ge(r_ok, SEQS - 1)
            transpose_numerators(SEQS - 1, 1)
            transpose_output(PAIRS - 1)


def block_c(nc, X, ident, WCh, WCl, a, out):
    with ExitStack() as ctx:
        def sb(name, shape, dt=F32):
            return ctx.enter_context(nc.sbuf_tensor("c_" + name, shape, dt))

        def sem(name):
            return ctx.enter_context(nc.semaphore("c_" + name))

        NG = E + 1
        LO = 32
        zhat = sb("zhat", [P, GT, D])
        stats = sb("stats", [P, GT, 6])
        mv = sb("mv", [P, GT, 2])
        rstd = sb("rstd", [P, GT])
        half = sb("half", [P, GT])
        zTh = sb("zth", [P, KT, GN], F16)
        zTl = sb("ztl", [P, KT, GN], F16)
        hTh = sb("hth", [P, MT, GN], F16)
        hTl = sb("htl", [P, MT, GN], F16)
        th = sb("th", [P, 2, GN])
        gs = sb("gs", [P, 2, GN])
        gu = sb("gu", [P, 2, GN])
        hs = sb("hs", [P, 2, GN])
        lg = sb("lg", [P, GT, NG])
        before = sb("before", [P, E, E])
        above = sb("above", [P, GT, E, E])
        ties = sb("ties", [P, GT, E, E])
        rank = sb("rank", [P, GT, E])
        top = sb("top", [P, GT])
        ex = sb("ex", [P, GT, E])
        gate = sb("gate", [P, GT, 1])
        den = sb("den", [P, 2, GT])
        cmb = sb("cmb", [P, GT, 2, LO])
        cT = sb("ct", [P, GN], F16)
        sel = sb("sel", [P, HID], F16)
        B = [ctx.enter_context(nc.psum_tensor(f"c_bank{n}", [P, 512], F32)) for n in range(8)]

        cst_in, init = sem("cst_in"), sem("init")
        ln_st, ln_mv, ln_add, ln_rs, z_ok, z_tr = (sem(n) for n in ("ln_st", "ln_mv", "ln_add", "ln_rs", "z_ok", "z_tr"))
        zT_hi, zT_lo = sem("zt_hi"), sem("zt_lo")
        g_mm, u_mm, c_mm = sem("g_mm"), sem("u_mm"), sem("c_mm")
        th_ok, gs_ok, gu_ok, hs_ok, h_hi, h_lo = (sem(n) for n in ("th_ok", "gs_ok", "gu_ok", "hs_ok", "h_hi", "h_lo"))
        dn, x_new, stored = sem("dn"), sem("x_new"), sem("stored")
        rt_mm, lg_ok, route, ex_ok, gate_ok, cmb_ok = (sem(n) for n in ("rt_mm", "lg_ok", "route", "ex_ok", "gate_ok", "cmb_ok"))
        rel_ok = sem("rel_ok")
        c_tr, cT_hi, cT_lo = sem("c_tr"), sem("ct_hi"), sem("ct_lo")

        block = ctx.enter_context(nc.Block())
        SETUP = (init, 3)
        LAST = GROUPS - 1
        assert E * I_MOE % P == 0
        WT = E * I_MOE // P + 1
        NR = 9

        def in_loop(eng, body):
            body(0, False)
            with eng.Fori(1, LAST) as i:
                body(i, False)
            body(LAST, True)

        def tiles(group):
            return [X[:, bass.ds(GT * group + j, 1), :].rearrange("p o d -> p (o d)") for j in range(GT)]

        def wcols(off, n):
            return tuple(w[:, :, :].rearrange("p c n -> p (c n)")[:, off:off + n] for w in (WCh, WCl))

        @block.sync
        def _(sp):
            sp.dma_start(sel[:, :], a["sel"]).then_inc(cst_in, 16)
            sp.dma_start(before[:, :, :], a["before"].rearrange("p (e f) -> p e f", e=E)).then_inc(cst_in, 16)

            def body(i, last):
                sp.wait_ge(x_new, GT * i + GT)
                og = out.rearrange("(g t p) d -> g p t d", p=P, t=GT)
                sp.dma_start(og[bass.ds(i, 1)].rearrange("o p t d -> (o p) t d"), X[:, bass.ds(GT * i, GT), :]).then_inc(stored, 16)

            in_loop(sp, body)
            sp.wait_ge(stored, 16 * GROUPS)

        @block.gpsimd
        def _(pool):
            nc.gpsimd.memset(half[:, :], -0.5).then_inc(init, 1)
            nc.gpsimd.memset(cmb[:, :, :, :], 0.0).then_inc(init, 1)
            nc.gpsimd.memset(cT[:, :], 0.0).then_inc(init, 1)
            pool.wait_ge(init, 3)
            ln_rstd(nc, pool, mv, rstd, half[:, :], ln_mv, GT, ln_add, 1, ln_rs, SETUP)

            def body(i, last):
                for m in range(MT):
                    n = MT * i + m
                    pool.wait_ge(h_hi, n + 1)
                    if m == 0:
                        pool.wait_ge(dn, GT * i)
                    nc.gpsimd.tensor_tensor(hTl[:, m], hs[:, m % 2], hTh[:, m], ALU.subtract).then_inc(h_lo, 1)
                    if m == MT // 2 and not last:
                        used = (z_ok, GT * i + GT)
                        ln_rstd(nc, pool, mv, rstd, half[:, :], ln_mv, GT * i + 2 * GT, ln_add, i + 2, ln_rs, SETUP, waits=[used])

            in_loop(pool, body)

        @block.scalar
        def _(act):
            def zT_hi_parts(g):
                for kt in range(KT):
                    act.wait_ge(z_tr, KT * g + kt + 1)
                    nc.scalar.activation(zTh[:, kt], B[kt][:, :], ACT.Copy, scale=S_X).then_inc(zT_hi, 1)

            def route_exps(g):
                act.wait_ge(rel_ok, g + 1)
                nc.scalar.activation(ex[:, :, :], ex[:, :, :], ACT.Exp).then_inc(ex_ok, 1)
                nc.scalar.activation(gate[:, :, :], lg[:, :, E:NG], ACT.Tanh, scale=0.5).then_inc(gate_ok, 1)

            def cT_hi_part(g):
                act.wait_ge(c_tr, g + 1)
                nc.scalar.activation(cT[0:2 * LO, :], B[3][0:2 * LO, :], ACT.Copy, scale=S_CMB).then_inc(cT_hi, 1)

            zT_hi_parts(0)
            route_exps(0)
            act.wait_ge(init, 3)
            cT_hi_part(0)

            def body(i, last):
                def tanh(m):
                    n = MT * i + m
                    act.wait_ge(g_mm, n + 1)
                    if m >= 2:
                        act.wait_ge(gs_ok, n - 1)
                    nc.scalar.activation(th[:, m % 2], B[m % 2][:, :], ACT.Tanh, scale=0.5 / (S_X * S_W)).then_inc(th_ok, 1)

                def hidden_hi(m):
                    n = MT * i + m
                    if m == 0:
                        act.wait_ge(dn, GT * i)
                    act.wait_ge(hs_ok, n + 1)
                    nc.scalar.activation(hTh[:, m], hs[:, m % 2], ACT.Copy).then_inc(h_hi, 1)

                act.wait_ge(gs_ok, MT * i)
                tanh(0)
                for m in range(1, MT):
                    tanh(m)
                    hidden_hi(m - 1)
                hidden_hi(MT - 1)
                if not last:
                    zT_hi_parts(i + 1)
                    route_exps(i + 1)
                    cT_hi_part(i + 1)

            in_loop(act, body)

        @block.vector
        def _(dve):
            def normalise(g):
                dve.wait_ge(ln_rs, g + 1)
                for j, src in enumerate(tiles(g)):
                    ln_normalise(nc, dve, src, zhat[:, j, :], mv, rstd, j, z_ok)

            def zT_lo_parts(g):
                for kt in range(KT):
                    dve.wait_ge(zT_hi, KT * g + kt + 1)
                    nc.vector.scalar_tensor_tensor(zTl[:, kt], B[kt][:, :], S_X, zTh[:, kt], ALU.mult, ALU.subtract).then_inc(zT_lo, 1)

            def routing(g):
                dve.wait_ge(rt_mm, g + 1)
                nc.vector.tensor_scalar(lg[:, :, :], B[2][:, 0:GT * NG].rearrange("p (t e) -> p t e", e=NG),
                                        1.0 / (S_X * S_W), None, ALU.mult).then_inc(lg_ok, 1)
                dve.wait_ge(lg_ok, g + 1)
                l = lg[:, :, 0:E]
                nc.vector.tensor_reduce(out=top[:, :].unsqueeze(2), in_=l, axis=AX.X, op=ALU.max).then_inc(route, 1)
                dve.wait_ge(route, NR * g + 1)
                nc.vector.tensor_tensor(ex[:, :, :], l, top[:, :].unsqueeze(2).to_broadcast([P, GT, E]), ALU.subtract).then_inc(rel_ok, 1)
                one, two = l.unsqueeze(3).to_broadcast([P, GT, E, E]), l.unsqueeze(2).to_broadcast([P, GT, E, E])
                nc.vector.tensor_tensor(ties[:, :, :, :], two, one, ALU.is_equal).then_inc(route, 1)
                nc.vector.tensor_tensor(above[:, :, :, :], two, one, ALU.is_gt).then_inc(route, 1)
                dve.wait_ge(route, NR * g + 2)
                nc.vector.tensor_tensor(ties[:, :, :, :], ties[:, :, :, :], before[:, :, :].unsqueeze(1).to_broadcast([P, GT, E, E]),
                                        ALU.mult).then_inc(route, 1)
                dve.wait_ge(route, NR * g + 4)
                nc.vector.tensor_tensor(above[:, :, :, :], above[:, :, :, :], ties[:, :, :, :], ALU.add).then_inc(route, 1)
                dve.wait_ge(route, NR * g + 5)
                nc.vector.tensor_reduce(out=rank[:, :, :].unsqueeze(3), in_=above[:, :, :, :], axis=AX.X, op=ALU.add).then_inc(route, 1)
                dve.wait_ge(route, NR * g + 6)
                dve.wait_ge(ex_ok, g + 1)
                nc.vector.scalar_tensor_tensor(ex[:, :, :], rank[:, :, :], 2.0, ex[:, :, :], ALU.is_lt, ALU.mult).then_inc(route, 1)
                dve.wait_ge(route, NR * g + 7)
                nc.vector.tensor_reduce(out=den[:, 0, :].unsqueeze(2), in_=ex[:, :, :], axis=AX.X, op=ALU.add).then_inc(route, 1)
                dve.wait_ge(route, NR * g + 8)
                nc.vector.reciprocal(den[:, 1, :], den[:, 0, :]).then_inc(route, 1)
                dve.wait_ge(route, NR * g + 9)
                dve.wait_ge(c_tr, g)
                dve.wait_ge(gate_ok, g + 1)
                for copy in range(2):
                    nc.vector.tensor_tensor(cmb[:, :, copy, 0:E], ex[:, :, :], den[:, 1, :].unsqueeze(2).to_broadcast([P, GT, E]), ALU.mult)
                    ins = nc.vector.tensor_scalar(cmb[:, :, copy, E:NG], gate[:, :, :], 0.5, 0.5, ALU.mult, ALU.add)
                ins.then_inc(cmb_ok, 1)

            def cT_lo_part(g):
                dve.wait_ge(cT_hi, g + 1)
                lo = cT[LO:2 * LO, :]
                nc.vector.scalar_tensor_tensor(lo, B[3][LO:2 * LO, :], S_CMB, lo, ALU.mult, ALU.subtract).then_inc(cT_lo, 1)

            ln_statistics(nc, dve, tiles(0), mv, stats, ln_st, ln_mv, 0, SETUP)
            normalise(0)
            zT_lo_parts(0)
            dve.wait_ge(cst_in, 32)
            dve.wait_ge(init, 3)
            routing(0)
            cT_lo_part(0)

            def body(i, last):
                def hidden(m):
                    n, b = MT * i + m, m % 2
                    dve.wait_ge(th_ok, n + 1)
                    dve.wait_ge(gu_ok, n)
                    nc.vector.scalar_tensor_tensor(gs[:, b], th[:, b], 1.0, B[b][:, :], ALU.add, ALU.mult).then_inc(gs_ok, 1)
                    dve.wait_ge(gs_ok, n + 1)
                    dve.wait_ge(u_mm, n + 1)
                    nc.vector.tensor_tensor(gu[:, b], gs[:, b], B[2 + b][:, :], ALU.mult).then_inc(gu_ok, 1)
                    dve.wait_ge(gu_ok, n + 1)
                    c = min(m, WT - 1)
                    dve.wait_ge(c_mm, WT * i + c + 1)
                    if m >= 2:
                        dve.wait_ge(h_lo, n - 1)
                    else:
                        dve.wait_ge(h_lo, MT * i)
                    scale = 0.5 / (S_X * S_W) ** 2 * S_H / S_CMB
                    nc.vector.scalar_tensor_tensor(hs[:, b], gu[:, b], scale, B[4 + c % 2][:, :], ALU.mult, ALU.mult).then_inc(hs_ok, 1)

                def add_output(j):
                    dve.wait_ge(dn, GT * i + j + 1)
                    xj = tiles(i)[j]
                    nc.vector.scalar_tensor_tensor(xj, B[6 + j % 2][:, 0:D], 1.0 / (S_H * S_W), xj, ALU.mult, ALU.add).then_inc(x_new, 1)

                for m in range(MT):
                    hidden(m)
                    if m == MT // 2 - 2 and not last:
                        ln_statistics(nc, dve, tiles(i + 1), mv, stats, ln_st, ln_mv, i + 1, SETUP)
                    if m == MT // 2 + 2 and not last:
                        normalise(i + 1)
                add_output(0)
                if not last:
                    zT_lo_parts(i + 1)
                add_output(1)
                if not last:
                    routing(i + 1)
                add_output(2)
                add_output(3)
                if not last:
                    cT_lo_part(i + 1)

            in_loop(dve, body)

        @block.tensor
        def _(pe):
            def transpose_z(g):
                for j in range(GT):
                    pe.wait_ge(z_ok, GT * g + j + 1)
                    for kt in range(KT):
                        ins = nc.tensor.transpose(B[kt][:, j * P:(j + 1) * P], zhat[:, j, kt * P:(kt + 1) * P], ident[:, :])
                        if j == GT - 1:
                            ins.then_inc(z_tr, 1)

            def router(g):
                pe.wait_ge(zT_lo, KT * g + KT)
                for j in range(GT):
                    for kt in range(KT):
                        z = (zTh[:, kt, j * P:(j + 1) * P], zTl[:, kt, j * P:(j + 1) * P])
                        ins = matmul3(nc, B[2][:, NG * j:NG * j + NG], z, wcols(RT_OFF + NG * kt, NG), kt == 0, kt == KT - 1)
                ins.then_inc(rt_mm, 1)

            def transpose_weights(g):
                wait_apart(pe, SETUP, (cmb_ok, g + 1))
                pe.wait_ge(*SETUP)
                for j in range(GT):
                    ins = nc.tensor.transpose(B[3][0:2 * LO, j * P:(j + 1) * P], cmb[:, j].rearrange("p a c -> p (a c)"), ident[:, :])
                ins.then_inc(c_tr, 1)

            transpose_z(0)
            router(0)
            pe.wait_ge(cst_in, 32)

            def body(i, last):
                def gate_up(m):
                    n = MT * i + m
                    for bank, off, done, read in ((m % 2, 0, g_mm, gs_ok), (2 + m % 2, HID, u_mm, gu_ok)):
                        pe.wait_ge(read, n - 1 if m >= 2 else MT * i)
                        for kt in range(KT):
                            w = wcols(GU_OFF + kt * 2 * HID + off + m * P, P)
                            ins = matmul3(nc, B[bank][:, :], w, (zTh[:, kt], zTl[:, kt]), kt == 0, kt == KT - 1)
                        ins.then_inc(done, 1)
                    if m >= WT:
                        return
                    if m == 0:
                        if isinstance(i, int) and i == 0:
                            transpose_weights(0)
                        pe.wait_ge(cT_lo, i + 1)
                    pe.wait_ge(hs_ok, n - 1 if m >= 2 else MT * i)
                    nc.tensor.matmul(B[4 + m % 2][:, :], sel[:, m * P:(m + 1) * P], cT[:, :], start=True, stop=True).then_inc(c_mm, 1)

                def down(j):
                    pe.wait_ge(x_new, GT * i + j - 1 if j >= 2 else GT * i)
                    for m in range(MT):
                        if j == 0:
                            pe.wait_ge(h_lo, MT * i + m + 1)
                        h = (hTh[:, m, j * P:(j + 1) * P], hTl[:, m, j * P:(j + 1) * P])
                        ins = matmul3(nc, B[6 + j % 2][:, 0:D], h, wcols(DN_OFF + m * D, D), m == 0, m == MT - 1)
                    ins.then_inc(dn, 1)

                pe.wait_ge(zT_lo, KT * i + KT)
                pe.wait_ge(lg_ok, i + 1)
                for m in range(MT):
                    gate_up(m)
                down(0)
                if not last:
                    pe.wait_ge(gs_ok, MT * i + MT)
                    transpose_z(i + 1)
                down(1)
                if not last:
                    pe.wait_ge(gu_ok, MT * i + MT)
                    router(i + 1)
                down(2)
                down(3)
                if not last:
                    transpose_weights(i + 1)

            in_loop(pe, body)


def build(nc, a, out, phases="ABC"):
    with ExitStack() as ctx:
        X = ctx.enter_context(nc.sbuf_tensor("x_res", [P, TILES, D], F32))
        ident = ctx.enter_context(nc.sbuf_tensor("ident", [P, P], F32))
        block_a(nc, X, ident, a)
        if "B" in phases:
            WCh = ctx.enter_context(nc.sbuf_tensor("wc_hi", [P, WC_CHUNKS, CH], F16))
            WCl = ctx.enter_context(nc.sbuf_tensor("wc_lo", [P, WC_CHUNKS, CH], F16))
            block_b(nc, X, ident, WCh, WCl, a)
        if "C" in phases:
            block_c(nc, X, ident, WCh, WCl, a, out)
        else:
            with nc.semaphore("dbg") as dbg, nc.Block() as block:
                @block.sync
                def _(sp):
                    sp.dma_start(out.rearrange("(t p) d -> p t d", p=P), X[:, :, :]).then_inc(dbg, 16)
                    sp.wait_ge(dbg, 16)


def rope_tables():
    inv = (np.float32(1.0) / np.float32(10000.0) ** (np.arange(0, HD, 2, dtype=np.float32) / np.float32(HD))).astype(np.float32)
    ang = np.arange(L, dtype=np.float32)[:, None] * inv[None, :]
    ang = np.concatenate([ang, ang], axis=-1).astype(np.float64)
    return np.cos(ang), np.sin(ang)


def constants():
    cos, sin = rope_tables()
    q = 1.0 / (S_X * S_W * np.sqrt(float(HD)))
    tabq = np.concatenate([cos.T * q, np.roll(sin, -1, axis=1).T * q], axis=1)
    k = 1.0 / (S_X * S_W)
    tabk = np.concatenate([np.tile(cos * k, (2, 1)), np.tile(sin * k, (2, 1))], axis=1)
    mask = np.zeros((P, 2), np.float32)
    r = np.arange(P) % 32
    mask[:, 0] = np.where((r >= XD) & (r < 2 * XD), 1, 0)
    mask[:, 1] = np.where((r >= 2 * XD) & (r < 3 * XD), 1, 0)
    sel = np.zeros((P, HID), np.float16)
    for n in range(E * I_MOE + I_SH):
        e = min(n // I_MOE, E)
        sel[e, n] = sel[32 + e, n] = 1
    before = np.tile(np.tril(np.ones((E, E), np.float32), -1).reshape(1, E * E), (P, 1))
    return {"maskB": mask, "sel": sel, "before": before, "tabq": tabq.astype(np.float32), "tabk": tabk.astype(np.float32), "ident": np.eye(P, dtype=np.float32)}


def layout(x, ctx_2048, L0_attn_Wq, L0_attn_Wk, L0_attn_Wv, L0_attn_Wo, L0_xattn_gamma, L0_ffn_router_weight,
           L0_ffn_gate_up_proj, L0_ffn_down_proj, L0_ffn_sh_gate_w, L0_ffn_sh_up_w, L0_ffn_sh_down_w, L0_ffn_shared_gate_w):
    arr = {"x": x.reshape(T, D)}

    def by_kt(w):
        return w.reshape(KT, P, -1).transpose(1, 0, 2).reshape(P, -1)

    chunks = [by_kt(L0_attn_Wk), by_kt(L0_attn_Wv)]
    chunks += [by_kt(L0_attn_Wq[:, c * 512:(c + 1) * 512]) for c in range(4)]
    wo = L0_attn_Wo.reshape(H, HD, D).transpose(1, 0, 2)
    chunks += [wo[:, 4 * c:4 * c + 4].reshape(P, CH) for c in range(4)]
    arr["wA"] = np.stack(chunks)
    c = ctx_2048.reshape(TILES, 2, XS, XJ, XD, D)
    st = np.zeros((TILES, XJ, 32, 2, XS, D), np.float32)
    for n in range(3):
        st[:, :, XD * n:XD * n + XD] = c.transpose(0, 3, 4, 1, 2, 5)
    st[:, :, MAXROW] = S_Y
    arr["ctxS"] = st.reshape(TILES, P, 2 * XS, D)
    arr["ctxT"] = ctx_2048.reshape(TILES, 2, 64, 2, P).transpose(0, 4, 3, 1, 2).reshape(TILES, P, 2 * 2 * 64)
    arr["gamma"] = L0_xattn_gamma.reshape(1, 1)
    gate = np.concatenate([L0_ffn_gate_up_proj[:, :I_MOE].reshape(-1, D), L0_ffn_sh_gate_w])
    up = np.concatenate([L0_ffn_gate_up_proj[:, I_MOE:].reshape(-1, D), L0_ffn_sh_up_w])
    down = np.concatenate([L0_ffn_down_proj.transpose(0, 2, 1).reshape(-1, D), L0_ffn_sh_down_w.T])
    pad = np.zeros((HID - gate.shape[0], D), np.float32)
    gu = np.concatenate([gate, pad, up, pad]).T
    dn = np.concatenate([down, pad]).reshape(MT, P, D).transpose(1, 0, 2).reshape(P, -1)
    rt = by_kt(np.concatenate([L0_ffn_router_weight, L0_ffn_shared_gate_w]).T)
    wc = np.concatenate([by_kt(gu), dn, rt], axis=1)
    wc = np.concatenate([wc, np.zeros((P, WC_CHUNKS * CH - wc.shape[1]), np.float32)], axis=1)
    arr["wC"] = wc.reshape(P, WC_CHUNKS, CH).transpose(1, 0, 2)
    arr.update(constants())
    return arr


def kernel(**inputs):
    import concourse.bacc as bacc
    from concourse.bass_utils import run_bass_kernel_spmd

    nc = bacc.Bacc("TRN2", target_bir_lowering=False, num_devices=1)
    arrays = {k: np.ascontiguousarray(v) for k, v in layout(**{k: np.asarray(v) for k, v in inputs.items()}).items()}
    aps = {k: nc.dram_tensor("in_" + k, v.shape, mybir.dt.from_np(v.dtype), kind="ExternalInput").ap() for k, v in arrays.items()}
    out = nc.dram_tensor("out", (T, D), F32, kind="ExternalOutput").ap()
    build(nc, aps, out)
    r = run_bass_kernel_spmd(nc, [{"in_" + k: v for k, v in arrays.items()}], core_ids=[0])
    return r.results[0]["out"].reshape(SEQS, L, D)
```
